# Optimizing a Trainium2 kernel written in Bass

```python
import numpy as np
import jax
import jax.numpy as jnp

def _softmax(x, axis=-1):
    return jax.nn.softmax(x, axis=axis)

def _gelu(x):
    return jax.nn.gelu(x, approximate=True)

def _silu(x):
    return jax.nn.silu(x)

def _sigmoid(x):
    return jax.nn.sigmoid(x)

def _layernorm(x, axis=-1, eps=1e-05):
    m = jnp.mean(x, axis=axis, keepdims=True)
    v = jnp.var(x, axis=axis, keepdims=True)
    return (x - m) / jnp.sqrt(v + eps)

def _scatter_add(tgt, idx, src, axis=0):
    return tgt.at[idx].add(src)

def _segment_sum(src, seg, n):
    return jax.ops.segment_sum(src, seg, n)
kernel_name = 'mk_seq_postln_d1_jaxref_r4_6ea101'

def setup_inputs(seed: int=0):
    np.random.seed(seed)
    _w = jnp.asarray

    def _L0_attn_setup():
        import jax, jax.numpy as jnp
        import numpy as np
        D_MODEL = 512
        EXPAND = 2
        D_INNER = EXPAND * D_MODEL
        D_SSM = D_INNER
        D_STATE = 128
        NGROUPS = 1
        HEADDIM = 64
        NHEADS = D_SSM // HEADDIM
        D_CONV = 4
        CHUNK = 64
        CONV_DIM = D_SSM + 2 * NGROUPS * D_STATE
        D_IN_PROJ = 2 * D_INNER + 2 * NGROUPS * D_STATE + NHEADS
        EPS = 1e-05

        def silu(x):
            return x * jax.nn.sigmoid(x)

        def softplus(x):
            return jnp.log1p(jnp.exp(-jnp.abs(x))) + jnp.maximum(x, 0)

        def segsum(x):
            T = x.shape[-1]
            xe = jnp.broadcast_to(x[..., :, None], x.shape + (T,))
            mask_lo = jnp.tril(jnp.ones((T, T), dtype=bool), k=-1)
            xe = jnp.where(mask_lo, xe, 0.0)
            s = jnp.cumsum(xe, axis=-2)
            mask = jnp.tril(jnp.ones((T, T), dtype=bool), k=0)
            return jnp.where(mask, s, -jnp.inf)

        def ssd(x, A, B, C, chunk_size):
            b, s, h, p = x.shape
            c = s // chunk_size
            resh = lambda m: m.reshape((b, c, chunk_size) + m.shape[2:])
            x, A, B, C = (resh(x), resh(A), resh(B), resh(C))
            A = jnp.transpose(A, (0, 3, 1, 2))
            A_cumsum = jnp.cumsum(A, axis=-1)
            L = jnp.exp(segsum(A))
            Y_diag = jnp.einsum('bclhn,bcshn,bhcls,bcshp->bclhp', C, B, L, x)
            decay_states = jnp.exp(A_cumsum[..., -1:] - A_cumsum)
            states = jnp.einsum('bclhn,bhcl,bclhp->bchpn', B, decay_states, x)
            init = jnp.zeros_like(states[:, :1])
            states = jnp.concatenate([init, states], axis=1)
            A_last = jnp.pad(A_cumsum[:, :, :, -1], ((0, 0), (0, 0), (1, 0)))
            decay_chunk = jnp.exp(segsum(A_last))
            new_states = jnp.einsum('bhzc,bchpn->bzhpn', decay_chunk, states)
            states, final_state = (new_states[:, :-1], new_states[:, -1])
            state_decay_out = jnp.exp(A_cumsum)
            Y_off = jnp.einsum('bclhn,bchpn,bhcl->bclhp', C, states, state_decay_out)
            Y = (Y_diag + Y_off).reshape(b, s, h, p)
            return (Y, final_state)
        key = jax.random.key(seed)
        ks = jax.random.split(key, 8)
        u = jax.random.normal(ks[0], (2, 1024, D_MODEL), dtype=jnp.float32)
        W_in = jax.random.normal(ks[1], (D_MODEL, D_IN_PROJ), dtype=jnp.float32) * D_MODEL ** (-0.5)
        conv_w = jax.random.uniform(ks[2], (D_CONV, CONV_DIM), dtype=jnp.float32, minval=-0.1, maxval=0.1)
        conv_b = jnp.zeros((CONV_DIM,), dtype=jnp.float32)
        dt = jnp.exp(jax.random.uniform(ks[3], (NHEADS,)) * (np.log(0.1) - np.log(0.001)) + np.log(0.001))
        dt = jnp.clip(dt, 0.0001)
        dt_bias = dt + jnp.log(jnp.expm1(dt))
        A_log = jnp.log(jax.random.uniform(ks[4], (NHEADS,), minval=1.0, maxval=16.0))
        D = jnp.ones((NHEADS,), dtype=jnp.float32)
        norm_scale = jnp.ones((D_SSM,), dtype=jnp.float32)
        W_out = jax.random.normal(ks[5], (D_INNER, D_MODEL), dtype=jnp.float32) * D_INNER ** (-0.5)
        return {'u': u, 'W_in': W_in, 'conv_w': conv_w, 'conv_b': conv_b, 'dt_bias': dt_bias, 'A_log': A_log, 'D': D, 'norm_scale': norm_scale, 'W_out': W_out}
    _L0_attn_in = _L0_attn_setup()

    def _L0_ffn_setup():
        import jax, jax.numpy as jnp
        import numpy as np
        from jax import lax
        D_MODEL = 512
        D_CROSS = 2048
        D_RETR = 128
        D_PRIV = 256
        N_EXPERTS = 4096
        N_HEADS = 8
        K_PER_HEAD = 8
        NUM_KEYS = int(np.sqrt(N_EXPERTS))
        BATCH, SEQ = (2, 512)
        key = jax.random.key(seed)
        ks = jax.random.split(key, 10)
        s = 0.02
        return {'hidden_states': jax.random.normal(ks[0], (BATCH, SEQ, D_MODEL), jnp.float32), 'W_up': jax.random.normal(ks[1], (D_CROSS, D_MODEL), jnp.float32) * s, 'b_up': jnp.zeros((D_CROSS,), jnp.float32), 'W_down': jax.random.normal(ks[2], (D_PRIV, D_CROSS), jnp.float32) * s, 'b_down': jnp.zeros((D_PRIV,), jnp.float32), 'W_q': jax.random.normal(ks[3], (D_RETR * N_HEADS, D_PRIV), jnp.float32) * s, 'keys': jax.random.normal(ks[4], (N_HEADS, NUM_KEYS, 2, D_RETR // 2), jnp.float32) * s, 'down_embed': jax.random.normal(ks[5], (N_EXPERTS, D_PRIV), jnp.float32) * s, 'up_embed': jax.random.normal(ks[6], (N_EXPERTS, D_MODEL), jnp.float32) * s}
    _L0_ffn_in = _L0_ffn_setup()
    _d = {'L0_attn_u': _L0_attn_in['u'], 'L0_attn_W_in': _L0_attn_in['W_in'], 'L0_attn_conv_w': _L0_attn_in['conv_w'], 'L0_attn_conv_b': _L0_attn_in['conv_b'], 'L0_attn_dt_bias': _L0_attn_in['dt_bias'], 'L0_attn_A_log': _L0_attn_in['A_log'], 'L0_attn_D': _L0_attn_in['D'], 'L0_attn_norm_scale': _L0_attn_in['norm_scale'], 'L0_attn_W_out': _L0_attn_in['W_out'], 'L0_ffn_W_up': _L0_ffn_in['W_up'], 'L0_ffn_b_up': _L0_ffn_in['b_up'], 'L0_ffn_W_down': _L0_ffn_in['W_down'], 'L0_ffn_b_down': _L0_ffn_in['b_down'], 'L0_ffn_W_q': _L0_ffn_in['W_q'], 'L0_ffn_keys': _L0_ffn_in['keys'], 'L0_ffn_down_embed': _L0_ffn_in['down_embed'], 'L0_ffn_up_embed': _L0_ffn_in['up_embed']}
    _x0 = _d['L0_attn_u']
    _d['L0_attn_u'] = jax.random.normal(jax.random.fold_in(jax.random.key(seed), 1), (1, 4096, 512), dtype=_x0.dtype)
    del _x0
    return _d

def reference(L0_attn_u, L0_attn_W_in, L0_attn_conv_w, L0_attn_conv_b, L0_attn_dt_bias, L0_attn_A_log, L0_attn_D, L0_attn_norm_scale, L0_attn_W_out, L0_ffn_W_up, L0_ffn_b_up, L0_ffn_W_down, L0_ffn_b_down, L0_ffn_W_q, L0_ffn_keys, L0_ffn_down_embed, L0_ffn_up_embed):

    def _L0_attn_ref(u, W_in, conv_w, conv_b, dt_bias, A_log, D, norm_scale, W_out):
        import jax, jax.numpy as jnp
        import numpy as np
        D_MODEL = 512
        EXPAND = 2
        D_INNER = EXPAND * D_MODEL
        D_SSM = D_INNER
        D_STATE = 128
        NGROUPS = 1
        HEADDIM = 64
        NHEADS = D_SSM // HEADDIM
        D_CONV = 4
        CHUNK = 64
        CONV_DIM = D_SSM + 2 * NGROUPS * D_STATE
        D_IN_PROJ = 2 * D_INNER + 2 * NGROUPS * D_STATE + NHEADS
        EPS = 1e-05

        def silu(x):
            return x * jax.nn.sigmoid(x)

        def softplus(x):
            return jnp.log1p(jnp.exp(-jnp.abs(x))) + jnp.maximum(x, 0)

        def segsum(x):
            T = x.shape[-1]
            xe = jnp.broadcast_to(x[..., :, None], x.shape + (T,))
            mask_lo = jnp.tril(jnp.ones((T, T), dtype=bool), k=-1)
            xe = jnp.where(mask_lo, xe, 0.0)
            s = jnp.cumsum(xe, axis=-2)
            mask = jnp.tril(jnp.ones((T, T), dtype=bool), k=0)
            return jnp.where(mask, s, -jnp.inf)

        def ssd(x, A, B, C, chunk_size):
            b, s, h, p = x.shape
            c = s // chunk_size
            resh = lambda m: m.reshape((b, c, chunk_size) + m.shape[2:])
            x, A, B, C = (resh(x), resh(A), resh(B), resh(C))
            A = jnp.transpose(A, (0, 3, 1, 2))
            A_cumsum = jnp.cumsum(A, axis=-1)
            L = jnp.exp(segsum(A))
            Y_diag = jnp.einsum('bclhn,bcshn,bhcls,bcshp->bclhp', C, B, L, x)
            decay_states = jnp.exp(A_cumsum[..., -1:] - A_cumsum)
            states = jnp.einsum('bclhn,bhcl,bclhp->bchpn', B, decay_states, x)
            init = jnp.zeros_like(states[:, :1])
            states = jnp.concatenate([init, states], axis=1)
            A_last = jnp.pad(A_cumsum[:, :, :, -1], ((0, 0), (0, 0), (1, 0)))
            decay_chunk = jnp.exp(segsum(A_last))
            new_states = jnp.einsum('bhzc,bchpn->bzhpn', decay_chunk, states)
            states, final_state = (new_states[:, :-1], new_states[:, -1])
            state_decay_out = jnp.exp(A_cumsum)
            Y_off = jnp.einsum('bclhn,bchpn,bhcl->bclhp', C, states, state_decay_out)
            Y = (Y_diag + Y_off).reshape(b, s, h, p)
            return (Y, final_state)
        b, s, _ = u.shape
        zxbcdt = u @ W_in
        z, xBC, dt = jnp.split(zxbcdt, [D_INNER, D_INNER + D_SSM + 2 * NGROUPS * D_STATE], axis=-1)
        xp = jnp.pad(xBC, ((0, 0), (D_CONV - 1, 0), (0, 0)))
        conv = conv_b
        for i in range(D_CONV):
            conv = conv + xp[:, i:i + s, :] * conv_w[i]
        xBC = silu(conv)
        x, B, C = jnp.split(xBC, [D_SSM, D_SSM + NGROUPS * D_STATE], axis=-1)
        x = x.reshape(b, s, NHEADS, HEADDIM)
        dt = softplus(dt + dt_bias)
        A = -jnp.exp(A_log)
        Bh = jnp.broadcast_to(B[:, :, None, :], (b, s, NHEADS, D_STATE))
        Ch = jnp.broadcast_to(C[:, :, None, :], (b, s, NHEADS, D_STATE))
        y, _final = ssd(x * dt[..., None], A * dt, Bh, Ch, CHUNK)
        y = y + x * D[None, None, :, None]
        y = y.reshape(b, s, D_SSM)
        y = y * silu(z)
        var = jnp.mean(jnp.square(y), axis=-1, keepdims=True)
        y = y * jax.lax.rsqrt(var + EPS) * norm_scale
        return y @ W_out

    def _L0_ffn_ref(hidden_states, W_up, b_up, W_down, b_down, W_q, keys, down_embed, up_embed):
        import jax, jax.numpy as jnp
        import numpy as np
        from jax import lax
        D_MODEL = 512
        D_CROSS = 2048
        D_RETR = 128
        D_PRIV = 256
        N_EXPERTS = 4096
        N_HEADS = 8
        K_PER_HEAD = 8
        NUM_KEYS = int(np.sqrt(N_EXPERTS))
        BATCH, SEQ = (2, 512)
        b, t, _ = hidden_states.shape
        act = jax.nn.silu
        h = act(jnp.einsum('btd,cd->btc', hidden_states, W_up) + b_up)
        h = jnp.einsum('btc,pc->btp', h, W_down) + b_down
        q = jnp.einsum('btp,rp->btr', h, W_q)
        q = q.reshape(b, t, 2, N_HEADS, D_RETR // 2).transpose(2, 0, 1, 3, 4)
        sim = jnp.einsum('pbthn,hkpn->pbthk', q, keys)
        scores, idx = lax.top_k(sim, K_PER_HEAD)
        sx, sy = (scores[0], scores[1])
        ix, iy = (idx[0], idx[1])
        all_scores = (sx[..., :, None] + sy[..., None, :]).reshape(b, t, N_HEADS, K_PER_HEAD * K_PER_HEAD)
        all_indices = (ix[..., :, None] * NUM_KEYS + iy[..., None, :]).reshape(b, t, N_HEADS, K_PER_HEAD * K_PER_HEAD)
        sc, pk = lax.top_k(all_scores, K_PER_HEAD)
        indices = jnp.take_along_axis(all_indices, pk, axis=-1)
        de = down_embed[indices]
        ue = up_embed[indices]
        z = jnp.einsum('btd,bthkd->bthk', h, de)
        z = act(z * jax.nn.softmax(sc, axis=-1))
        out = jnp.einsum('bthk,bthkd->btd', z, ue)
        return out
    x = L0_attn_u
    x = _layernorm(x + _L0_attn_ref(x, L0_attn_W_in, L0_attn_conv_w, L0_attn_conv_b, L0_attn_dt_bias, L0_attn_A_log, L0_attn_D, L0_attn_norm_scale, L0_attn_W_out), axis=-1)
    x = _layernorm(x + _L0_ffn_ref(x, L0_ffn_W_up, L0_ffn_b_up, L0_ffn_W_down, L0_ffn_b_down, L0_ffn_W_q, L0_ffn_keys, L0_ffn_down_embed, L0_ffn_up_embed), axis=-1)
    return x

_drawn_inputs = setup_inputs


def setup_inputs(seed=0):
    import zlib

    import numpy as np

    out = dict(_drawn_inputs(seed))
    spreads = {'L0_attn_conv_b': (0.0, 0.1),
     'L0_attn_D': (1.0, 0.2),
     'L0_attn_norm_scale': (1.0, 0.2),
     'L0_ffn_b_up': (0.0, 0.8),
     'L0_ffn_b_down': (0.0, 0.8)}
    factors = {'L0_attn_dt_bias': 8.0,
     'L0_attn_A_log': 8.0,
     'L0_ffn_W_up': 8.0,
     'L0_ffn_W_down': 8.0,
     'L0_ffn_W_q': 8.0,
     'L0_ffn_keys': 8.0,
     'L0_ffn_down_embed': 8.0,
     'L0_ffn_up_embed': 8.0}
    for name, (base, spread) in spreads.items():
        noise = np.random.default_rng([zlib.crc32(name.encode()), seed]).standard_normal(out[name].shape)
        drawn = base * np.exp(spread * noise) if base else spread * noise
        out[name] = jnp.asarray(drawn.astype(out[name].dtype))
    for name, factor in factors.items():
        out[name] = (out[name] * factor).astype(out[name].dtype)
    return out
```

```python
from contextlib import ExitStack

import numpy as np

import concourse.bass as bass
from concourse import mybir

F32 = mybir.dt.float32
U32 = mybir.dt.uint32
ALU = mybir.AluOpType
ACT = mybir.ActivationFunctionType
AX = mybir.AxisListType

P = 128
T = 4096
D = 512
DI = 1024
NS = 128
NH = 16
HD = 64
TAPS = 4
CONV = DI + 2 * NS
DPROJ = 2 * DI + 2 * NS + NH
DC = 2048
DP = 256
EH = 8
TOP = 8
NK = 64
HALF = 64
NE = NK * NK
ROW = DP + D
NT = T // P
KD = D // P
KC = CONV // P
KX = DI // P
KU = DC // P
KP = DP // P
RING = 8
PICKS = EH * TOP
NG = 2 * EH
DTB = 8
EPS = 1e-5
BANK = 512


def build(nc, uT, u, W_in, W_out, W_upT, W_downT, W_q, keysT, embed, consts, iota8, conv_w, conv_b,
          dt_bias, A_log, D_cols, norm_cols, b_up, b_down, out):
    with ExitStack() as ctx:
        def sb(name, shape, dt=F32):
            return ctx.enter_context(nc.sbuf_tensor(name, shape, dt))

        def sem(name):
            return ctx.enter_context(nc.semaphore(name))

        w_in = sb("w_in", [P, KD, DPROJ])
        w_out = sb("w_out", [P, KX, D])
        w_up = sb("w_up", [P, KD, DC])
        w_down = sb("w_down", [P, KU, DP])
        w_key = sb("w_key", [P, KP, NG * NK])
        cst = sb("cst", [P, 4, P])
        ident, later, upto, ones = (cst[:, n, :] for n in range(4))
        diag_d = sb("diag_d", [P, KX, P])
        iota = sb("iota", [P, TOP])
        taps = sb("taps", [P, KC, TAPS])
        cbias = sb("cbias", [P, KC])
        dcol = sb("dcol", [P, KX])
        ncol = sb("ncol", [P, KX])
        bup = sb("bup", [P, KU])
        bdown = sb("bdown", [P, DP])
        small = sb("small", [P, 3, NH])
        steps = sb("steps", [P, NT, 2, NH])
        epsc = sb("epsc", [P, 1])
        ring = sb("ring", [P, RING, ROW])
        ut = sb("ut", [P, KD, P])
        u_tok = sb("u_tok", [P, D])
        raw = sb("raw", [P, KC, TAPS - 1 + P])
        xc = sb("xc", [P, KC, P])
        zs = sb("zs", [P, DI])
        cur = sb("cur", [P, 2, NH])
        decay = sb("decay", [P, 2, NH])
        seg = sb("seg", [P, NH, P])
        bcb = sb("bcb", [P, 2, P])
        btok, cbm = bcb[:, 0, :], bcb[:, 1, :]
        xdt = sb("xdt", [P, DI])
        xdec = sb("xdec", [P, DI])
        state = sb("state", [P, DI])
        yoff = sb("yoff", [P, DI])
        x1 = sb("x1", [P, D])
        x1T = sb("x1T", [P, KD, P])
        h = sb("h", [P, DP])
        hT = sb("hT", [P, KP, P])
        st6 = sb("st6", [P, 6])
        mv = sb("mv", [P, 2])
        sm = sb("sm", [P, 8])
        v1 = sb("v1", [P, NG, TOP])
        i1 = sb("i1", [P, NG, TOP], U32)
        allsc = sb("allsc", [P, EH, TOP * TOP])
        hot = sb("hot", [P, PICKS, TOP])
        v2 = sb("v2", [P, EH, TOP])
        pk = sb("pk", [P, EH, TOP], U32)
        ak = sb("ak", [P, PICKS], U32)
        bk = sb("bk", [P, PICKS], U32)
        ixy = sb("ixy", [P, 2, PICKS])
        idx = sb("idx", [P, PICKS], U32)
        prob = sb("prob", [P, EH, TOP])
        psm = sb("psm", [P, 2, EH])
        hcur = sb("hcur", [P, DP])
        acc = sb("acc", [P, 2, D])
        dots = sb("dots", [P, PICKS])
        zp = sb("zp", [P, PICKS])
        coef = sb("coef", [P, PICKS])
        st6b = sb("st6b", [P, 6])
        mvb = sb("mvb", [P, 2])
        smb = sb("smb", [P, 2])

        y = xdt
        yT = xdec
        obuf = hot[:, :, :].rearrange("p a b -> p (a b)")
        h1T = seg
        bank = [ctx.enter_context(nc.psum_tensor(f"bank{n}", [P, BANK], F32)) for n in range(8)]

        wq_stage = ring[0:HALF, :, :].rearrange("p a b -> p (a b)")[:, 0:NG * DP]\
            .rearrange("p (g c) -> p g c", g=NG)
        key_stage = ring[0:HALF, :, :].rearrange("p a b -> p (a b)")[:, NG * DP:NG * DP + NG * NK]\
            .rearrange("p (g c) -> p g c", g=NG)
        u_stage = ring[:, :, :].rearrange("p a b -> p (a b)")[:, 0:DTB * D].rearrange("p (t k c) -> p t k c", t=DTB, k=KD)

        w_small = sem("w_small")
        w_in_in, w_out_in, w_up_in, w_down_in, wq_in = (
            sem(n) for n in ("w_in_in", "w_out_in", "w_up_in", "w_down_in", "wq_in"))
        ublk_in, ut_in, utok_in = sem("ublk_in"), sem("ut_in"), sem("utok_in")
        row_in = [sem(f"row_in{n}") for n in range(RING)]
        out_done = sem("out_done")
        zeroed, const_made, expa_made = sem("zeroed"), sem("const_made"), sem("expa_made")
        keyw_mm, keyw_out = sem("keyw_mm"), sem("keyw_out")
        dt_mm, dt_raw, dt_act, dt_dve = sem("dt_mm"), sem("dt_raw"), sem("dt_act"), sem("dt_dve")
        xbc_mm, z_mm, seg_mm, xT_mm, cb_mm, yoff_mm, y_mm, st_mm = (
            sem(n) for n in ("xbc_mm", "z_mm", "seg_mm", "xT_mm", "cb_mm", "yoff_mm", "y_mm", "st_mm"))
        yT_mm, op_mm, x1T_mm, h1_mm, hp_mm, hT_mm, sim_mm = (
            sem(n) for n in ("yT_mm", "op_mm", "x1T_mm", "h1_mm", "hp_mm", "hT_mm", "sim_mm"))
        hist_ok, raw_ok, tap_ok, xc_ok, z_ok, cur_ok, am_ok, e_ok, dec_ok = (
            sem(n) for n in ("hist_ok", "raw_ok", "tap_ok", "xc_ok", "z_ok", "cur_ok", "am_ok", "e_ok", "dec_ok"))
        yT_ok, rms_ok, ln_ok, x1T_ok, h1_ok, hT_ok, exp_ok, hcur_ok, coef_ok, ln2_ok = (
            sem(n) for n in ("yT_ok", "rms_ok", "ln_ok", "x1T_ok", "h1_ok", "hT_ok", "exp_ok", "hcur_ok",
                             "coef_ok", "ln2_ok"))
        sq_ok = sem("sq_ok")
        conv_ok, cbm_ok, xdt_ok, g_ok, xdec_ok, y_ok, st_ok, bn_ok, x1_ok, h_ok = (
            sem(n) for n in ("conv_ok", "cbm_ok", "xdt_ok", "g_ok", "xdec_ok", "y_ok", "st_ok", "bn_ok", "x1_ok", "h_ok"))
        top1_ok, top2_ok, idx_ok, soft_ok, dot_ok, zp_ok, row_used, sum_ok, o_ok = (
            sem(n) for n in ("top1_ok", "top2_ok", "idx_ok", "soft_ok", "dot_ok", "zp_ok", "row_used", "sum_ok", "o_ok"))
        act_fence, dve_fence, pool_fence, sp_fence = sem("act_fence"), sem("dve_fence"), sem("pool_fence"), sem("sp_fence")

        block = ctx.enter_context(nc.Block())

        @block.sync
        def _(sp):
            sp.dma_start(cst[:, :, :], consts).then_inc(w_small, 16)
            sp.dma_start(iota[:, :], iota8).then_inc(w_small, 16)
            sp.dma_start(taps[:, :, :], conv_w).then_inc(w_small, 16)
            sp.dma_start(cbias[:, :], conv_b).then_inc(w_small, 16)
            sp.dma_start(dcol[:, :], D_cols).then_inc(w_small, 16)
            sp.dma_start(ncol[:, :], norm_cols).then_inc(w_small, 16)
            sp.dma_start(bup[:, :], b_up).then_inc(w_small, 16)
            sp.dma_start(bdown[:, :], b_down).then_inc(w_small, 16)
            sp.dma_start(small[:, 0, :], dt_bias).then_inc(w_small, 16)
            sp.dma_start(small[:, 1, :], A_log).then_inc(w_small, 16)
            sp.dma_start(wq_stage, W_q.rearrange("(g n) c -> n g c", n=HALF)).then_inc(wq_in, 16)
            sp.dma_start(key_stage, keysT).then_inc(wq_in, 16)
            sp.dma_start(w_in[:, :, :], W_in.rearrange("(k p) n -> p k n", p=P)).then_inc(w_in_in, 16)
            sp.wait_ge(keyw_mm, 4)
            sp.dma_start(u_stage, uT[0:DTB].rearrange("t p (k c) -> p t k c", k=KD)).then_inc(ublk_in, 16)
            sp.dma_start(ut[:, :, :], uT[0].rearrange("p (k c) -> p k c", k=KD)).then_inc(ut_in, 16)
            sp.dma_start(u_tok[:, :], u[0]).then_inc(utok_in, 16)
            sp.dma_start(w_out[:, :, :], W_out.rearrange("(k p) n -> p k n", p=P)).then_inc(w_out_in, 16)
            sp.dma_start(w_up[:, :, :], W_upT.rearrange("(k p) n -> p k n", p=P)).then_inc(w_up_in, 16)
            sp.dma_start(w_down[:, :, :], W_downT.rearrange("(k p) n -> p k n", p=P)).then_inc(w_down_in, 16)
            for b in range(1, NT // DTB):
                sp.wait_ge(dt_mm, b)
                sp.dma_start(u_stage, uT[b * DTB:(b + 1) * DTB].rearrange("t p (k c) -> p t k c", k=KD))\
                    .then_inc(ublk_in, 16)
            with sp.Fori(1, NT) as i:
                sp.wait_ge(z_mm, i * 2)
                sp.sem_inc(sp_fence, 1)
                sp.dma_start(ut[:, :, :], uT[bass.ds(i, 1)].rearrange("t p (k c) -> p (t k) c", k=KD))\
                    .then_inc(ut_in, 16)
                sp.wait_ge(bn_ok, i * 4 - 3)
                sp.sem_inc(sp_fence, 1)
                sp.dma_start(u_tok[:, :], u[bass.ds(i, 1)].rearrange("t p c -> p (t c)")).then_inc(utok_in, 16)
            sp.wait_ge(out_done, 16 * NT + 16)

        @block.gpsimd
        def _(pool):
            pool.memset(epsc[:, :], EPS).then_inc(zeroed, 1)
            pool.wait_ge(zeroed, 1)
            pool.memset(epsc[:, :], EPS).then_inc(out_done, 16)
            pool.memset(state[:, :], 0.0).then_inc(zeroed, 1)
            pool.memset(raw[:, :, 0:TAPS - 1], 0.0).then_inc(zeroed, 1)

            def gathers(t, first):
                pool.wait_ge(idx_ok, t + 1)
                for s in range(EH):
                    for r in range(RING):
                        k = s * RING + r
                        if not (first and k < RING):
                            pool.wait_ge(row_used, PICKS * t + (k - RING + 1))
                            pool.sem_inc(pool_fence, 1)
                        pool.indirect_dma_start(
                            out=ring[:, r, :], out_offset=None, in_=embed,
                            in_offset=bass.IndirectOffsetOnAxis(ap=idx[:, k:k + 1], axis=0))\
                            .then_inc(row_in[r], 16)

            gathers(0, True)
            with pool.Fori(1, NT) as t:
                gathers(t, False)

        @block.tensor
        def _(pe):
            pe.wait_ge(wq_in, 32)
            for c in range(KP):
                for b in range(2):
                    for g in range(8):
                        gg = b * 8 + g
                        m = pe.matmul(bank[2 * c + b][:, g * NK:(g + 1) * NK], wq_stage[:, gg, c * P:(c + 1) * P],
                                      key_stage[:, gg, :], start=True, stop=True)
                    m.then_inc(keyw_mm, 1)
            pe.wait_ge(w_in_in, 16)
            for b in range(NT // DTB):
                pe.wait_ge(ublk_in, 16 * (b + 1))
                for j in range(DTB):
                    for k in range(KD):
                        m = pe.matmul(bank[4 + b][:, j * NH:(j + 1) * NH], u_stage[:, j, k, :],
                                      w_in[:, k, DPROJ - NH:DPROJ], start=(k == 0), stop=(k == KD - 1))
                m.then_inc(dt_mm, 1)
            pe.wait_ge(w_small, 160)
            pe.wait_ge(keyw_out, 4)
            pe.wait_ge(dt_raw, NT // DTB)
            pe.wait_ge(zeroed, 3)
            pe.wait_ge(const_made, KX + KX)

            def front(i, first):
                pe.wait_ge(ut_in, 16 * i + 16)
                if not first:
                    pe.wait_ge(st_ok, 2 * i)
                    pe.wait_ge(h1_ok, KU * i)
                    pe.wait_ge(h_ok, i)
                for c in range(KC):
                    for k in range(KD):
                        m = pe.matmul(bank[c // 4][:, (c % 4) * P:(c % 4 + 1) * P],
                                      w_in[:, k, DI + c * P:DI + (c + 1) * P], ut[:, k, :],
                                      start=(k == 0), stop=(k == KD - 1))
                    if c in (3, 7, KC - 1):
                        m.then_inc(xbc_mm, 1)
                if not first:
                    pe.wait_ge(hT_ok, i)
                    pe.wait_ge(bn_ok, 4 * i - 3)
                for b in range(2):
                    for k in range(KD):
                        m = pe.matmul(bank[3 + b][:, :], ut[:, k, :], w_in[:, k, b * BANK:(b + 1) * BANK],
                                      start=(k == 0), stop=(k == KD - 1))
                    m.then_inc(z_mm, 1)
                if not first:
                    pe.wait_ge(x1T_ok, i)
                for b, at in enumerate((5, 0, 1, 2)):
                    pe.wait_ge(am_ok, 4 * i + b + 1)
                    if at != 5:
                        pe.wait_ge(tap_ok, KC * i + min(4 * at + 4, KC))
                    pe.matmul(bank[at][:, :], later, seg[:, 4 * b:4 * b + 4, :],
                              start=True, stop=True).then_inc(seg_mm, 1)
                pe.wait_ge(xc_ok, i + 1)
                if not first:
                    pe.wait_ge(top1_ok, 3 * i)
                for c in range(KX):
                    m = pe.transpose(bank[6 + c // 4][:, (c % 4) * P:(c % 4 + 1) * P], xc[:, c, :], ident)
                    if c % 4 == 3:
                        m.then_inc(xT_mm, 1)
                pe.wait_ge(z_ok, 2 * i + 2)
                pe.transpose(bank[3][:, 0:P], xc[:, KX, :], ident)
                pe.matmul(bank[3][:, P:2 * P], xc[:, KX, :], xc[:, KX + 1, :], start=True, stop=True)
                pe.matmul(bank[3][:, 2 * P:2 * P + NH], upto, cur[:, 1, :], start=True, stop=True)
                pe.matmul(bank[3][:, 3 * P:3 * P + NH], ones, cur[:, 1, :], start=True, stop=True)\
                    .then_inc(cb_mm, 1)
                if not first:
                    pe.wait_ge(st_ok, 2 * i)
                pe.wait_ge(e_ok, 4 * i + 1)
                for b in range(2):
                    pe.matmul(bank[4 + b][:, :], xc[:, KX + 1, :], state[:, b * BANK:(b + 1) * BANK],
                              start=True, stop=True).then_inc(yoff_mm, 1)
                pe.wait_ge(xdt_ok, 2 * i + 2)
                pe.wait_ge(g_ok, i + 1)
                for c in range(KX):
                    col = slice((c % 4) * P, (c % 4 + 1) * P)
                    pe.matmul(bank[6 + c // 4][:, col], xc[:, c, :], diag_d[:, c, :], start=(c % 4 == 0), stop=False,
                              skip_group_check=True)
                    for j in range(2):
                        hh = 2 * c + j
                        a = (c % 4) * P + j * HD
                        m = pe.matmul(bank[6 + c // 4][:, a:a + HD], seg[:, hh, :], xdt[:, hh * HD:(hh + 1) * HD],
                                      start=False, stop=(c % 4 == 3 and j == 1), skip_group_check=True)
                    if c % 4 == 3:
                        m.then_inc(y_mm, 1)
                pe.wait_ge(xdec_ok, i + 1)
                pe.wait_ge(dec_ok, 3 * i + 3)
                pe.wait_ge(e_ok, 4 * i + 4)
                for b in range(2):
                    pe.matmul(bank[b][:, :], btok[:, :], xdec[:, b * BANK:(b + 1) * BANK],
                              start=True, stop=True).then_inc(st_mm, 1)
                pe.wait_ge(y_ok, 4 * i + 4)
                for c in range(KX):
                    m = pe.transpose(bank[2 + c // 4][:, (c % 4) * P:(c % 4 + 1) * P], y[:, c * P:(c + 1) * P], ident)
                    if c % 4 == 3:
                        m.then_inc(yT_mm, 1)
                for c in range(KX):
                    if c % 4 == 0:
                        pe.wait_ge(yT_ok, 2 * i + c // 4 + 1)
                    m = pe.matmul(bank[4][:, :], yT[:, c * P:(c + 1) * P], w_out[:, c, :],
                                  start=(c == 0), stop=(c == KX - 1))
                m.then_inc(op_mm, 1)
                pe.wait_ge(x1_ok, i + 1)
                for k in range(KD):
                    m = pe.transpose(bank[5][:, k * P:(k + 1) * P], x1[:, k * P:(k + 1) * P], ident)
                m.then_inc(x1T_mm, 1)
                pe.wait_ge(x1T_ok, i + 1)
                pe.wait_ge(st_ok, 2 * i + 2)
                for c in range(KU):
                    at = (6, 7, 0, 1)[c // 4]
                    for k in range(KD):
                        m = pe.matmul(bank[at][:, (c % 4) * P:(c % 4 + 1) * P], w_up[:, k, c * P:(c + 1) * P],
                                      x1T[:, k, :], start=(k == 0), stop=(k == KD - 1))
                    if c % 4 == 3:
                        m.then_inc(h1_mm, 1)
                for c in range(KU):
                    if c % 4 == 0:
                        pe.wait_ge(h1_ok, KU * i + c + 4)
                    m = pe.matmul(bank[2][:, 0:DP], h1T[:, c, :], w_down[:, c, :],
                                  start=(c == 0), stop=(c == KU - 1))
                m.then_inc(hp_mm, 1)
                pe.wait_ge(h_ok, i + 1)
                for c in range(KP):
                    m = pe.transpose(bank[3][:, c * P:(c + 1) * P], h[:, c * P:(c + 1) * P], ident)
                m.then_inc(hT_mm, 1)
                pe.wait_ge(hT_ok, i + 1)
                for b in range(2):
                    for c in range(KP):
                        m = pe.matmul(bank[6 + b][:, :], hT[:, c, :], w_key[:, c, b * BANK:(b + 1) * BANK],
                                      start=(c == 0), stop=(c == KP - 1))
                m.then_inc(sim_mm, 1)

            pe.wait_ge(w_out_in, 16)
            pe.wait_ge(w_up_in, 16)
            pe.wait_ge(w_down_in, 16)
            front(0, True)
            with pe.Fori(1, NT) as i:
                front(i, False)

        @block.scalar
        def _(act):
            act.wait_ge(w_small, 160)
            act.activation(small[:, 2, :], small[:, 1, :], ACT.Exp).then_inc(expa_made, 1)
            act.wait_ge(dt_raw, NT // DTB)
            sp_x = hot[:, :, :].rearrange("p a b -> p (a b)")
            sp_e = allsc[:, :, :].rearrange("p a b -> p (a b)")
            act.activation(sp_e, sp_x, ACT.Abs).then_inc(dt_act, 1)
            act.wait_ge(dt_act, 1)
            act.activation(sp_e, sp_e, ACT.Exp, scale=-1.0).then_inc(dt_act, 1)

            def coefs(t, s):
                act.wait_ge(zp_ok, EH * t + s + 1)
                act.activation(coef[:, s * TOP:(s + 1) * TOP], zp[:, s * TOP:(s + 1) * TOP], ACT.Silu)\
                    .then_inc(coef_ok, 1)

            def front_a(i, first):
                if first:
                    act.wait_ge(dt_dve, 17)
                else:
                    act.wait_ge(cb_mm, i)
                    act.wait_ge(xdt_ok, 2 * i)
                act.activation(cur[:, :, :], steps[:, bass.ds(i, 1), :, :].rearrange("p a b c -> p (a b) c"),
                               ACT.Copy).then_inc(cur_ok, 1)
                act.wait_ge(cur_ok, i + 1)
                if not first:
                    act.wait_ge(hp_mm, i)
                for hh in range(NH):
                    m = act.activation(seg[:, hh, :], upto, ACT.Copy, scale=cur[:, 1, hh:hh + 1])
                    if hh % 4 == 3:
                        m.then_inc(am_ok, 1)
                if not first:
                    act.wait_ge(conv_ok, KC * 3 * i)
                    act.activation(raw[:, :, 0:TAPS - 1], raw[:, :, P:P + TAPS - 1], ACT.Copy).then_inc(hist_ok, 1)
                    act.wait_ge(hist_ok, i)
                    act.wait_ge(y_mm, 2 * i)
                for b in range(3):
                    n = min(4, KC - 4 * b)
                    act.wait_ge(xbc_mm, 3 * i + b + 1)
                    act.activation(raw[:, 4 * b:4 * b + n, TAPS - 1:],
                                   bank[b][:, 0:n * P].rearrange("p (a c) -> p a c", a=n), ACT.Copy).then_inc(raw_ok, 1)
                    for c in range(4 * b, 4 * b + n):
                        act.activation(xc[:, c, :], bank[b][:, (c % 4) * P:(c % 4 + 1) * P], ACT.Identity,
                                       bias=cbias[:, c:c + 1], scale=taps[:, c, TAPS - 1:TAPS]).then_inc(tap_ok, 1)
                for b in range(2):
                    act.wait_ge(z_mm, 2 * i + b + 1)
                    if b == 0 and not first:
                        act.wait_ge(y_ok, 4 * i)
                    act.activation(zs[:, b * BANK:(b + 1) * BANK], bank[3 + b][:, :], ACT.Silu).then_inc(z_ok, 1)
                act.wait_ge(conv_ok, KC * 3 * (i + 1))
                act.activation(xc[:, :, :], xc[:, :, :], ACT.Silu).then_inc(xc_ok, 1)
                for b, at in enumerate((5, 0, 1, 2)):
                    act.wait_ge(seg_mm, 4 * i + b + 1)
                    act.activation(seg[:, 4 * b:4 * b + 4, :],
                                   bank[at][:, :].rearrange("p (a c) -> p a c", a=4), ACT.Exp).then_inc(e_ok, 1)
                act.wait_ge(cb_mm, i + 1)
                act.activation(decay[:, 0, :], bank[3][:, 2 * P:2 * P + NH], ACT.Exp).then_inc(dec_ok, 1)
                act.activation(decay[:, 1, :], bank[3][:, 3 * P:3 * P + NH], ACT.Exp).then_inc(dec_ok, 1)
                if not first:
                    act.wait_ge(st_mm, 2 * i)
                    act.wait_ge(g_ok, i)
                act.activation(bcb[:, :, :], bank[3][:, 0:2 * P].rearrange("p (a c) -> p a c", a=2), ACT.Copy).then_inc(dec_ok, 1)

            def front_b(i):
                act.wait_ge(y_ok, 4 * i + 4)
                act.activation(yoff[:, :], y[:, :], ACT.Square, accum_out=sm[:, 0:1]).then_inc(sq_ok, 1)
                for b in range(2):
                    act.wait_ge(yT_mm, 2 * i + b + 1)
                    if b == 0:
                        act.wait_ge(st_mm, 2 * i + 2)
                    act.activation(yT[:, b * BANK:(b + 1) * BANK], bank[2 + b][:, :], ACT.Copy).then_inc(yT_ok, 1)
                act.wait_ge(sq_ok, i + 1)
                act.activation(sm[:, 1:2], sm[:, 0:1], ACT.Sqrt, scale=1.0 / DI, bias=epsc[:, :]).then_inc(rms_ok, 1)

            def front_c(i):
                act.wait_ge(bn_ok, 4 * i + 3)
                act.activation(sm[:, 3:4], mv[:, 1:2], ACT.Sqrt, bias=epsc[:, :]).then_inc(ln_ok, 1)

            def front_d(i):
                act.wait_ge(x1T_mm, i + 1)
                act.activation(x1T[:, :, :], bank[5][:, :].rearrange("p (a c) -> p a c", a=KD), ACT.Copy)\
                    .then_inc(x1T_ok, 1)

            def front_e(i, b):
                act.wait_ge(h1_mm, 4 * i + b + 1)
                if b == 0:
                    act.wait_ge(y_mm, 2 * i + 2)
                for c in range(4 * b, 4 * b + 4):
                    act.activation(h1T[:, c, :], bank[(6, 7, 0, 1)[b]][:, (c % 4) * P:(c % 4 + 1) * P], ACT.Silu,
                                   bias=bup[:, c:c + 1]).then_inc(h1_ok, 1)

            def front_f(i):
                act.wait_ge(hT_mm, i + 1)
                act.activation(hT[:, :, :], bank[3][:, 0:DP].rearrange("p (a c) -> p a c", a=KP), ACT.Copy)\
                    .then_inc(hT_ok, 1)

            def front_g(i):
                act.wait_ge(soft_ok, 4 * i + 1)
                act.activation(prob[:, :, :], prob[:, :, :], ACT.Exp).then_inc(exp_ok, 1)

            def back_sqrt(t):
                act.wait_ge(sum_ok, 3 * t + 3)
                act.activation(smb[:, 0:1], mvb[:, 1:2], ACT.Sqrt, bias=epsc[:, :]).then_inc(ln2_ok, 1)

            def hand_over(i, first):
                act.wait_ge(h_ok, i + 1)
                if not first:
                    act.wait_ge(dot_ok, PICKS * i)
                act.activation(hcur[:, :], h[:, :], ACT.Copy).then_inc(hcur_ok, 1)
                if not first:
                    act.wait_ge(o_ok, i)
                act.activation(acc[:, 0, :], x1[:, :], ACT.Copy).then_inc(hcur_ok, 1)

            def store(t):
                act.wait_ge(o_ok, t + 1)
                act.sem_inc(act_fence, 1)
                act.dma_start(out[bass.ds(t, 1)].rearrange("t p c -> p (t c)"), obuf).then_inc(out_done, 16)

            front_a(0, True)
            front_b(0)
            front_c(0)
            front_d(0)
            for b in range(4):
                front_e(0, b)
            front_f(0)
            front_g(0)
            hand_over(0, True)
            with act.Fori(1, NT) as i:
                front_a(i, False)
                coefs(i - 1, 0)
                coefs(i - 1, 1)
                front_b(i)
                coefs(i - 1, 2)
                front_c(i)
                coefs(i - 1, 3)
                front_d(i)
                coefs(i - 1, 4)
                front_e(i, 0)
                front_e(i, 1)
                coefs(i - 1, 5)
                front_e(i, 2)
                front_e(i, 3)
                coefs(i - 1, 6)
                front_f(i)
                coefs(i - 1, 7)
                back_sqrt(i - 1)
                front_g(i)
                hand_over(i, False)
                store(i - 1)
            for s in range(EH):
                coefs(NT - 1, s)
            back_sqrt(NT - 1)
            act.wait_ge(o_ok, NT)
            act.dma_start(out[NT - 1], obuf).then_inc(out_done, 16)

        @block.vector
        def _(dve):
            dve.wait_ge(w_small, 160)
            for c in range(KX):
                dve.tensor_scalar(diag_d[:, c, :], ident, dcol[:, c:c + 1], None, ALU.mult).then_inc(const_made, 1)
            for c in range(2 * KP):
                dve.wait_ge(keyw_mm, c + 1)
                dve.tensor_copy(w_key[:, c // 2, (c % 2) * BANK:(c % 2 + 1) * BANK], bank[c][:, :]).then_inc(keyw_out, 1)
            sp_x = hot[:, :, :].rearrange("p a b -> p (a b)")
            sp_e = allsc[:, :, :].rearrange("p a b -> p (a b)")
            sp_r, sp_p = acc[:, 0, :], acc[:, 1, :]
            x_v = sp_x.rearrange("p (t n) -> p t n", n=NH)
            for b in range(NT // DTB):
                dve.wait_ge(dt_mm, b + 1)
                dve.tensor_tensor(x_v[:, b * DTB:(b + 1) * DTB, :],
                                  bank[4 + b][:, 0:DTB * NH].rearrange("p (t n) -> p t n", n=NH),
                                  small[:, 0:1, :].to_broadcast([P, DTB, NH]), ALU.add).then_inc(dt_raw, 1)
            dve.wait_ge(w_out_in, 16)
            for c in range(KX):
                dve.tensor_scalar(w_out[:, c, :], w_out[:, c, :], ncol[:, c:c + 1], None, ALU.mult)\
                    .then_inc(const_made, 1)
            dve.wait_ge(dt_act, 2)
            dve.tensor_scalar(sp_r, sp_e, 2.0, None, ALU.add).then_inc(dt_dve, 1)
            dve.wait_ge(dt_dve, 1)
            dve.reciprocal(sp_r, sp_r).then_inc(dt_dve, 1)
            dve.wait_ge(dt_dve, 2)
            dve.tensor_tensor(sp_r, sp_e, sp_r, ALU.mult).then_inc(dt_dve, 1)
            dve.wait_ge(dt_dve, 3)
            dve.tensor_tensor(sp_e, sp_r, sp_r, ALU.mult).then_inc(dt_dve, 1)
            dve.wait_ge(dt_dve, 4)
            dve.tensor_scalar(sp_p, sp_e, 1.0 / 17, None, ALU.mult).then_inc(dt_dve, 1)
            for n, odd in enumerate((15, 13, 11, 9, 7, 5, 3)):
                dve.wait_ge(dt_dve, 5 + n)
                dve.scalar_tensor_tensor(out=sp_p, in0=sp_p, scalar=1.0 / odd, in1=sp_e, op0=ALU.add, op1=ALU.mult)\
                    .then_inc(dt_dve, 1)
            dve.wait_ge(dt_dve, 12)
            dve.scalar_tensor_tensor(out=sp_p, in0=sp_p, scalar=1.0, in1=sp_r, op0=ALU.add, op1=ALU.mult)\
                .then_inc(dt_dve, 1)
            dve.tensor_scalar(sp_x, sp_x, 0.0, 0.5, ALU.max, ALU.mult).then_inc(dt_dve, 1)
            dve.wait_ge(dt_dve, 14)
            dve.tensor_tensor(sp_p, sp_p, sp_x, ALU.add).then_inc(dt_dve, 1)
            dve.wait_ge(dt_dve, 15)
            dve.wait_ge(expa_made, 1)
            p_v = sp_p.rearrange("p (t n) -> p t n", n=NH)
            dve.tensor_scalar(steps[:, :, 0, :], p_v, 2.0, None, ALU.mult).then_inc(dt_dve, 1)
            dve.scalar_tensor_tensor(out=steps[:, :, 1, :], in0=p_v, scalar=-2.0,
                                     in1=small[:, 2:3, :].to_broadcast([P, NT, NH]),
                                     op0=ALU.mult, op1=ALU.mult).then_inc(dt_dve, 1)
            dve.wait_ge(zeroed, 3)

            def convolve(i):
                for j in range(TAPS - 1):
                    for c in range(KC):
                        if j == 0:
                            dve.wait_ge(tap_ok, KC * i + c + 1)
                        else:
                            dve.wait_ge(conv_ok, KC * (3 * i + j - 1) + c + 1)
                        dve.scalar_tensor_tensor(out=xc[:, c, :], in0=raw[:, c, j:j + P], scalar=taps[:, c, j:j + 1],
                                                 in1=xc[:, c, :], op0=ALU.mult, op1=ALU.add).then_inc(conv_ok, 1)

            def heads(ap):
                return ap.rearrange("p (n c) -> p n c", c=HD)

            def scan_in(i, first):
                dve.wait_ge(dec_ok, 3 * i + 3)
                dve.tensor_tensor(cbm[:, :], cbm[:, :], upto, ALU.mult).then_inc(cbm_ok, 1)
                for b in range(2):
                    dve.wait_ge(xT_mm, 2 * i + b + 1)
                    if b == 0 and not first:
                        dve.wait_ge(yT_mm, 2 * i)
                        dve.wait_ge(sq_ok, i)
                    dve.tensor_tensor(heads(xdt[:, b * BANK:(b + 1) * BANK]), heads(bank[6 + b][:, :]),
                                      cur[:, 0, 8 * b:8 * b + 8].unsqueeze(2).to_broadcast([P, 8, HD]),
                                      ALU.mult).then_inc(xdt_ok, 1)
                dve.wait_ge(xdt_ok, 2 * i + 2)
                dve.wait_ge(e_ok, 4 * i + 4)
                if not first:
                    dve.wait_ge(op_mm, i)
                dve.tensor_tensor(heads(xdec[:, :]), heads(xdt[:, :]),
                                  seg[:, :, P - 1:P].to_broadcast([P, NH, HD]), ALU.mult).then_inc(xdec_ok, 1)
                dve.wait_ge(cbm_ok, i + 1)
                dve.wait_ge(xdec_ok, i + 1)
                dve.tensor_tensor(seg[:, :, :], seg[:, :, :], cbm[:, :].unsqueeze(1).to_broadcast([P, NH, P]),
                                  ALU.mult).then_inc(g_ok, 1)

            def scan_out(i):
                dve.wait_ge(yoff_mm, 2 * i + 2)
                dve.wait_ge(dec_ok, 3 * i + 3)
                for b in range(2):
                    dve.tensor_tensor(heads(yoff[:, b * BANK:(b + 1) * BANK]), heads(bank[4 + b][:, :]),
                                      decay[:, 0, 8 * b:8 * b + 8].unsqueeze(2).to_broadcast([P, 8, HD]),
                                      ALU.mult).then_inc(y_ok, 1)
                dve.tensor_tensor(heads(state[:, :]), heads(state[:, :]),
                                  decay[:, 1, :].unsqueeze(2).to_broadcast([P, NH, HD]), ALU.mult).then_inc(dve_fence, 1)
                dve.wait_ge(y_ok, 4 * i + 2)
                dve.wait_ge(y_mm, 2 * i + 2)
                for b in range(2):
                    dve.tensor_tensor(y[:, b * BANK:(b + 1) * BANK], yoff[:, b * BANK:(b + 1) * BANK], bank[6 + b][:, :],
                                      ALU.add).then_inc(y_half, 1)
                dve.wait_ge(z_ok, 2 * i + 2)
                for b in range(2):
                    dve.wait_ge(y_half, 2 * i + b + 1)
                    dve.tensor_tensor(y[:, b * BANK:(b + 1) * BANK], y[:, b * BANK:(b + 1) * BANK],
                                      zs[:, b * BANK:(b + 1) * BANK], ALU.mult).then_inc(y_ok, 1)
                dve.wait_ge(dve_fence, i + 1)
                for b in range(2):
                    dve.wait_ge(st_mm, 2 * i + b + 1)
                    dve.tensor_tensor(state[:, b * BANK:(b + 1) * BANK], state[:, b * BANK:(b + 1) * BANK],
                                      bank[b][:, :], ALU.add).then_inc(st_ok, 1)

            y_half = sem("y_half")

            def residual(i):
                dve.wait_ge(rms_ok, i + 1)
                dve.reciprocal(sm[:, 2:3], sm[:, 1:2]).then_inc(rr_ok, 1)
                dve.wait_ge(rr_ok, i + 1)
                dve.wait_ge(op_mm, i + 1)
                dve.wait_ge(utok_in, 16 * i + 16)
                dve.scalar_tensor_tensor(out=x1[:, :], in0=bank[4][:, :], scalar=sm[:, 2:3], in1=u_tok[:, :],
                                         op0=ALU.mult, op1=ALU.add).then_inc(bn_ok, 1)
                dve.wait_ge(bn_ok, 4 * i + 1)
                dve.bn_stats(st6[:, :], x1[:, :]).then_inc(bn_ok, 1)
                dve.wait_ge(bn_ok, 4 * i + 2)
                dve.sem_inc(fence, 1)
                dve.bn_aggr(mv[:, :], st6[:, :]).then_inc(bn_ok, 1)

            rr_ok = sem("rr_ok")
            fence = sem("fence")

            def norm1(i):
                dve.wait_ge(ln_ok, i + 1)
                dve.reciprocal(sm[:, 4:5], sm[:, 3:4]).then_inc(bn_ok, 1)
                dve.wait_ge(bn_ok, 4 * i + 4)
                dve.tensor_scalar(x1[:, :], x1[:, :], mv[:, 0:1], sm[:, 4:5], ALU.subtract, ALU.mult).then_inc(x1_ok, 1)

            def private(i, first):
                dve.wait_ge(hp_mm, i + 1)
                if not first:
                    dve.wait_ge(hcur_ok, 2 * i)
                dve.tensor_tensor(h[:, :], bank[2][:, 0:DP], bdown[:, :], ALU.add).then_inc(h_ok, 1)

            def top_halves(i):
                dve.wait_ge(sim_mm, i + 1)
                dve.sem_inc(fence, 1)
                for g in range(NG):
                    m = dve.max(out=v1[:, g, :], in_=bank[6 + g // 8][:, (g % 8) * NK:(g % 8 + 1) * NK])
                m.then_inc(top1_ok, 1)
                dve.wait_ge(top1_ok, 3 * i + 1)
                dve.sem_inc(fence, 1)
                for g in range(NG):
                    m = dve.max_index(i1[:, g, :], v1[:, g, :], bank[6 + g // 8][:, (g % 8) * NK:(g % 8 + 1) * NK])
                m.then_inc(top1_ok, 1)
                dve.tensor_tensor(allsc[:, :, :].rearrange("p n (a b) -> p n a b", a=TOP),
                                  v1[:, 0:EH, :].unsqueeze(3).to_broadcast([P, EH, TOP, TOP]),
                                  v1[:, EH:NG, :].unsqueeze(2).to_broadcast([P, EH, TOP, TOP]), ALU.add).then_inc(top1_ok, 1)

            def top_pairs(i, first):
                dve.wait_ge(top1_ok, 3 * i + 3)
                dve.sem_inc(fence, 1)
                for n in range(EH):
                    m = dve.max(out=v2[:, n, :], in_=allsc[:, n, :])
                m.then_inc(top2_ok, 1)
                dve.wait_ge(top2_ok, 4 * i + 1)
                dve.sem_inc(fence, 1)
                for n in range(EH):
                    m = dve.max_index(pk[:, n, :], v2[:, n, :], allsc[:, n, :])
                m.then_inc(top2_ok, 1)
                dve.tensor_tensor(prob[:, :, :], v2[:, :, :], v2[:, :, 0:1].to_broadcast([P, EH, TOP]), ALU.subtract)\
                    .then_inc(soft_ok, 1)
                dve.wait_ge(top2_ok, 4 * i + 2)
                pk_v = pk[:, :, :].rearrange("p a b -> p (a b)")
                dve.tensor_scalar(ak[:, :], pk_v, 3, None, ALU.logical_shift_right).then_inc(top2_ok, 1)
                dve.tensor_scalar(bk[:, :], pk_v, TOP - 1, None, ALU.bitwise_and).then_inc(top2_ok, 1)
                hot_x = allsc[:, :, :].rearrange("p n (k a) -> p n k a", a=TOP)
                if not first:
                    dve.wait_ge(out_done, 16 * i)
                hot_y = hot[:, :, :].rearrange("p (n k) a -> p n k a", n=EH)
                for n, (place, one) in enumerate(((ak, hot_x), (bk, hot_y))):
                    dve.wait_ge(top2_ok, 4 * i + 3 + n)
                    dve.tensor_tensor(one.rearrange("p n k a -> p (n k) a"),
                                      place[:, :].unsqueeze(2).to_broadcast([P, PICKS, TOP]),
                                      iota[:, :].unsqueeze(1).to_broadcast([P, PICKS, TOP]),
                                      ALU.is_equal).then_inc(dec1_ok, 1)
                for n, one in enumerate((hot_x, hot_y)):
                    dve.wait_ge(dec1_ok, 2 * i + n + 1)
                    dve.tensor_tensor(one, one, i1[:, n * EH:(n + 1) * EH, :].unsqueeze(2).to_broadcast([P, EH, TOP, TOP]),
                                      ALU.mult).then_inc(dec2_ok, 1)
                for n, one in enumerate((hot_x, hot_y)):
                    dve.wait_ge(dec2_ok, 2 * i + n + 1)
                    dve.tensor_reduce(ixy[:, n, :], one.rearrange("p n k a -> p (n k) a"), AX.X, ALU.add).then_inc(dec3_ok, 1)
                dve.wait_ge(dec3_ok, 2 * i + 2)
                dve.scalar_tensor_tensor(out=idx[:, :], in0=ixy[:, 0, :], scalar=float(NK), in1=ixy[:, 1, :],
                                         op0=ALU.mult, op1=ALU.add).then_inc(idx_ok, 1)

            dec1_ok, dec2_ok, dec3_ok = sem("dec1_ok"), sem("dec2_ok"), sem("dec3_ok")

            def softmax(i):
                dve.wait_ge(exp_ok, i + 1)
                dve.tensor_reduce(psm[:, 0, :], prob[:, :, :], AX.X, ALU.add).then_inc(soft_ok, 1)
                dve.wait_ge(soft_ok, 4 * i + 2)
                dve.reciprocal(psm[:, 1, :], psm[:, 0, :]).then_inc(soft_ok, 1)
                dve.wait_ge(soft_ok, 4 * i + 3)
                dve.tensor_tensor(prob[:, :, :], prob[:, :, :], psm[:, 1, :].unsqueeze(2).to_broadcast([P, EH, TOP]),
                                  ALU.mult).then_inc(soft_ok, 1)

            def experts(t, s):
                if s == 0:
                    dve.wait_ge(hcur_ok, 2 * t + 2)
                for r in range(TOP):
                    k = s * TOP + r
                    dve.wait_ge(row_in[r], 16 * (EH * t + s + 1))
                    dve.scalar_tensor_tensor(out=ring[:, r, 0:DP], in0=ring[:, r, 0:DP], scalar=1.0, in1=hcur[:, :],
                                             op0=ALU.mult, op1=ALU.mult, accum_out=dots[:, k:k + 1]).then_inc(dot_ok, 1)
                dve.wait_ge(dot_ok, PICKS * t + (s + 1) * TOP)
                if s == 0:
                    dve.wait_ge(soft_ok, 4 * t + 4)
                dve.tensor_tensor(zp[:, s * TOP:(s + 1) * TOP], dots[:, s * TOP:(s + 1) * TOP], prob[:, s, :], ALU.mult)\
                    .then_inc(zp_ok, 1)
                dve.wait_ge(coef_ok, EH * t + s + 1)
                for r in range(TOP):
                    k = s * TOP + r
                    if k >= 2:
                        dve.wait_ge(row_used, PICKS * t + k - 1)
                    if k == 1:
                        dve.tensor_scalar(acc[:, 1, :], ring[:, r, DP:ROW], coef[:, k:k + 1], None, ALU.mult)\
                            .then_inc(row_used, 1)
                    else:
                        dve.scalar_tensor_tensor(out=acc[:, r % 2, :], in0=ring[:, r, DP:ROW], scalar=coef[:, k:k + 1],
                                                 in1=acc[:, r % 2, :], op0=ALU.mult, op1=ALU.add).then_inc(row_used, 1)

            def back_stats(t):
                dve.wait_ge(row_used, PICKS * t + PICKS)
                dve.tensor_tensor(acc[:, 0, :], acc[:, 0, :], acc[:, 1, :], ALU.add).then_inc(sum_ok, 1)
                dve.wait_ge(sum_ok, 3 * t + 1)
                dve.bn_stats(st6b[:, :], acc[:, 0, :]).then_inc(sum_ok, 1)
                dve.wait_ge(sum_ok, 3 * t + 2)
                dve.sem_inc(fence, 1)
                dve.bn_aggr(mvb[:, :], st6b[:, :]).then_inc(sum_ok, 1)

            def back_norm(t):
                dve.wait_ge(ln2_ok, t + 1)
                dve.reciprocal(smb[:, 1:2], smb[:, 0:1]).then_inc(r2_ok, 1)
                dve.wait_ge(r2_ok, t + 1)
                dve.tensor_scalar(obuf, acc[:, 0, :], mvb[:, 0:1], smb[:, 1:2], ALU.subtract, ALU.mult)\
                    .then_inc(o_ok, 1)

            r2_ok = sem("r2_ok")

            convolve(0)
            scan_in(0, True)
            scan_out(0)
            residual(0)
            norm1(0)
            private(0, True)
            top_halves(0)
            top_pairs(0, True)
            softmax(0)

            def step(i):
                convolve(i)
                experts(i - 1, 0)
                scan_in(i, False)
                experts(i - 1, 1)
                scan_out(i)
                experts(i - 1, 2)
                residual(i)
                experts(i - 1, 3)
                norm1(i)
                experts(i - 1, 4)
                experts(i - 1, 5)
                private(i, False)
                experts(i - 1, 6)
                top_halves(i)
                experts(i - 1, 7)
                back_stats(i - 1)
                top_pairs(i, False)
                softmax(i)
                back_norm(i - 1)

            with dve.Fori(1, NT) as i:
                step(i)
            for s in range(EH):
                experts(NT - 1, s)
            back_stats(NT - 1)
            dve.wait_ge(out_done, 16 * NT)
            back_norm(NT - 1)


def kernel(L0_attn_u, L0_attn_W_in, L0_attn_conv_w, L0_attn_conv_b, L0_attn_dt_bias, L0_attn_A_log, L0_attn_D,
           L0_attn_norm_scale, L0_attn_W_out, L0_ffn_W_up, L0_ffn_b_up, L0_ffn_W_down, L0_ffn_b_down,
           L0_ffn_W_q, L0_ffn_keys, L0_ffn_down_embed, L0_ffn_up_embed):
    import concourse.bacc as bacc
    from concourse.bass_utils import run_bass_kernel_spmd

    def a(x):
        return np.asarray(x)

    def c(x):
        return np.ascontiguousarray(x)

    def rows(x):
        return c(np.broadcast_to(a(x)[None, :], (P, x.shape[0])))

    def cols(x, n):
        return c(a(x).reshape(n, P).T)

    u = a(L0_attn_u).reshape(NT, P, D)
    q = np.arange(P)
    consts = np.stack([q[:, None] == q[None, :], q[:, None] > q[None, :], q[:, None] <= q[None, :],
                       q[:, None] >= 0 * q[None, :]], 1).astype(np.float32)
    arrays = {
        "uT": c(u.reshape(NT, P, KD, P).transpose(0, 3, 2, 1).reshape(NT, P, D)),
        "u": c(u),
        "W_in": c(a(L0_attn_W_in)),
        "W_out": c(a(L0_attn_W_out)),
        "W_upT": c(a(L0_ffn_W_up).T),
        "W_downT": c(a(L0_ffn_W_down).T),
        "W_q": c(a(L0_ffn_W_q)),
        "keysT": c(a(L0_ffn_keys).transpose(3, 2, 0, 1).reshape(HALF, NG, NK)),
        "embed": c(np.concatenate([a(L0_ffn_down_embed), a(L0_ffn_up_embed)], 1)),
        "consts": consts,
        "iota8": c(np.broadcast_to(np.arange(TOP, dtype=np.float32), (P, TOP))),
        "conv_w": c(a(L0_attn_conv_w).reshape(TAPS, KC, P).transpose(2, 1, 0)),
        "conv_b": cols(L0_attn_conv_b, KC),
        "dt_bias": rows(L0_attn_dt_bias),
        "A_log": rows(L0_attn_A_log),
        "D_cols": cols(np.repeat(a(L0_attn_D), HD), KX),
        "norm_cols": cols(L0_attn_norm_scale, KX),
        "b_up": cols(L0_ffn_b_up, KU),
        "b_down": rows(L0_ffn_b_down),
    }
    nc = bacc.Bacc("TRN2", target_bir_lowering=False, num_devices=1)
    args = [nc.dram_tensor(n, x.shape, mybir.dt.from_np(x.dtype), kind="ExternalInput").ap() for n, x in arrays.items()]
    args.append(nc.dram_tensor("out", (NT, P, D), F32, kind="ExternalOutput").ap())
    build(nc, *args)
    r = run_bass_kernel_spmd(nc, [arrays], core_ids=[0])
    return r.results[0]["out"].reshape(1, T, D)
```

```python
from contextlib import ExitStack

import numpy as np

import concourse.bass as bass
from concourse import mybir

F32 = mybir.dt.float32
U32 = mybir.dt.uint32
ALU = mybir.AluOpType
ACT = mybir.ActivationFunctionType
AX = mybir.AxisListType

P = 128
T = 4096
D = 512
DI = 1024
NS = 128
NH = 16
HD = 64
TAPS = 4
CONV = DI + 2 * NS
DPROJ = 2 * DI + 2 * NS + NH
DC = 2048
DP = 256
EH = 8
TOP = 8
NK = 64
HALF = 64
NE = NK * NK
ROW = DP + D
NT = T // P
KD = D // P
KC = CONV // P
KX = DI // P
KU = DC // P
KP = DP // P
RING = 13
PICKS = EH * TOP
NG = 2 * EH
DTB = 8
EPS = 1e-5
BANK = 512
ON_PE = (2, 5)
DIAGS = 4
PE_ROWS = [k for k in range(PICKS) if k % TOP in ON_PE]
DVE_ROWS = [k for k in range(PICKS) if k % TOP not in ON_PE]


def build(nc, uT, u, W_in, W_out, W_upT, W_downT, W_q, keysT, embed, consts, iota8, conv_w, conv_b,
          dt_bias, A_log, D_cols, norm_cols, b_up, b_down, out):
    with ExitStack() as ctx:
        def sb(name, shape, dt=F32):
            return ctx.enter_context(nc.sbuf_tensor(name, shape, dt))

        def sem(name):
            return ctx.enter_context(nc.semaphore(name))

        w_in = sb("w_in", [P, KD, DPROJ])
        w_out = sb("w_out", [P, KX, D])
        w_up = sb("w_up", [P, KD, DC])
        w_down = sb("w_down", [P, KU, DP])
        w_key = sb("w_key", [P, KP, NG * NK])
        cst = sb("cst", [P, 4, P])
        ident, later, upto, ones = (cst[:, n, :] for n in range(4))
        diag_d = sb("diag_d", [P, KX, P])
        iota = sb("iota", [P, TOP])
        taps = sb("taps", [P, KC, TAPS])
        cbias = sb("cbias", [P, KC])
        dcol = sb("dcol", [P, KX])
        ncol = sb("ncol", [P, KX])
        bup = sb("bup", [P, KU])
        bdown = sb("bdown", [P, DP])
        small = sb("small", [P, 3, NH])
        steps = sb("steps", [P, NT, NH])
        epsc = sb("epsc", [P, 1])
        ring = sb("ring", [P, RING, ROW])
        ut = sb("ut", [P, D])
        raw = sb("raw", [P, KC, TAPS - 1 + P])
        xc = sb("xc", [P, KC, P])
        zs = sb("zs", [P, DI])
        cur = sb("cur", [P, 2, NH])
        decay = sb("decay", [P, 2, NH])
        seg = sb("seg", [P, NH, P])
        bcb = sb("bcb", [P, 2, P])
        xdt = sb("xdt", [P, DI])
        xdec = sb("xdec", [P, DI])
        state = sb("state", [P, DI])
        x1 = sb("x1", [P, D])
        st6 = sb("st6", [P, 6])
        mv = sb("mv", [P, 2])
        sm = sb("sm", [P, 8])
        v1 = sb("v1", [P, NG, TOP])
        i1 = sb("i1", [P, NG, TOP], U32)
        v2 = sb("v2", [P, EH, TOP])
        pk = sb("pk", [P, EH, TOP], U32)
        ak = sb("ak", [P, PICKS], U32)
        bk = sb("bk", [P, PICKS], U32)
        ixy = sb("ixy", [P, 2, PICKS])
        idx = sb("idx", [P, PICKS], U32)
        prob = sb("prob", [P, EH, TOP])
        psm = sb("psm", [P, 2, EH])
        hcur = sb("hcur", [P, DP])
        acc = sb("acc", [P, 2, D])
        dots = sb("dots", [P, PICKS])
        zp = sb("zp", [P, PICKS])
        coef = sb("coef", [P, PICKS])
        diag_c = sb("diag_c", [P, DIAGS, P])
        st6b = sb("st6b", [P, 6])
        mvb = sb("mvb", [P, 2])
        smb = sb("smb", [P, 2])

        uT_v = ut[:, :].rearrange("p (k c) -> p k c", k=KD)
        btok, cbm = bcb[:, 0, :], bcb[:, 1, :]
        y = xdt
        yT = xdec
        h1T = seg
        x1T = zs[:, 0:D].rearrange("p (k c) -> p k c", k=KD)
        h = zs[:, D:D + DP]
        hT = zs[:, D + DP:DI].rearrange("p (k c) -> p k c", k=KP)
        allsc = xdt[:, 0:BANK].rearrange("p (n c) -> p n c", n=EH)
        hot = xdt[:, BANK:DI].rearrange("p (k c) -> p k c", k=PICKS)
        obuf = xdt[:, BANK:DI]
        bank = [ctx.enter_context(nc.psum_tensor(f"bank{n}", [P, BANK], F32)) for n in range(8)]
        SUM = 5
        SEG_BANKS = (6, 0, 1, 2)
        UP_BANKS = (6, 7, 0, 3)

        stage = ring[:, :, :].rearrange("p a b -> p (a b)")
        WQ_END = NG * DP + NG * NK
        wq_stage = stage[0:HALF, 0:NG * DP].rearrange("p (g c) -> p g c", g=NG)
        key_stage = stage[0:HALF, NG * DP:WQ_END].rearrange("p (g c) -> p g c", g=NG)
        u_stage = [stage[:, a:a + DTB * D].rearrange("p (t k c) -> p t k c", t=DTB, k=KD) for a in (WQ_END, 0)]

        w_small, wdt_in = sem("w_small"), sem("wdt_in")
        w_in_in, w_out_in, w_up_in, w_down_in, wq_in = (
            sem(n) for n in ("w_in_in", "w_out_in", "w_up_in", "w_down_in", "wq_in"))
        ublk_in, ut_in, utok_in = [sem("ublk_in0"), sem("ublk_in1")], sem("ut_in"), sem("utok_in")
        row_in = [sem(f"row_in{n}") for n in range(RING)]
        out_done = sem("out_done")
        zeroed, const_made, expa_made = sem("zeroed"), sem("const_made"), sem("expa_made")
        keyw_mm, keyw_out = sem("keyw_mm"), sem("keyw_out")
        dt_mm, dt_raw, dt_act, dt_dve = sem("dt_mm"), sem("dt_raw"), sem("dt_act"), sem("dt_dve")
        xbc_mm, z_mm, seg_mm, xT_mm, cb_mm, yoff_mm, y_mm, st_mm = (
            sem(n) for n in ("xbc_mm", "z_mm", "seg_mm", "xT_mm", "cb_mm", "yoff_mm", "y_mm", "st_mm"))
        yT_mm, op_mm, x1T_mm, h1_mm, hp_mm, hT_mm, sim_mm, row_pe = (
            sem(n) for n in ("yT_mm", "op_mm", "x1T_mm", "h1_mm", "hp_mm", "hT_mm", "sim_mm", "row_pe"))
        hist_ok, raw_ok, tap_ok, xc_ok, z_ok, am_ok, e_ok, dec_ok = (
            sem(n) for n in ("hist_ok", "raw_ok", "tap_ok", "xc_ok", "z_ok", "am_ok", "e_ok", "dec_ok"))
        yT_ok, sq_ok, rms_ok, ln_ok, x1T_ok, h1_ok, hT_ok, exp_ok, hcur_ok, coef_ok, diag_ok, ln2_ok = (
            sem(n) for n in ("yT_ok", "sq_ok", "rms_ok", "ln_ok", "x1T_ok", "h1_ok", "hT_ok", "exp_ok", "hcur_ok",
                             "coef_ok", "diag_ok", "ln2_ok"))
        cur_ok, conv_ok, cbm_ok, xdt_ok, g_ok, xdec_ok, yoff_ok, y_half, y_ok, dcy_ok, st_ok, rr_ok, bn_ok, x1_ok, h_ok = (
            sem(n) for n in ("cur_ok", "conv_ok", "cbm_ok", "xdt_ok", "g_ok", "xdec_ok", "yoff_ok", "y_half", "y_ok",
                             "dcy_ok", "st_ok", "rr_ok", "bn_ok", "x1_ok", "h_ok"))
        top1_ok, top2_ok, hot_ok, pick_ok, ixy_ok, idx_ok, soft_ok, dot_ok, zp_ok, row_used, sum_ok, r2_ok, o_ok = (
            sem(n) for n in ("top1_ok", "top2_ok", "hot_ok", "pick_ok", "ixy_ok", "idx_ok", "soft_ok", "dot_ok",
                             "zp_ok", "row_used", "sum_ok", "r2_ok", "o_ok"))
        dve_fence, pool_fence, sp_fence = sem("dve_fence"), sem("pool_fence"), sem("sp_fence")

        block = ctx.enter_context(nc.Block())

        @block.sync
        def _(sp):
            def load_u_block(b):
                sp.dma_start(u_stage[b % 2], uT[b * DTB:(b + 1) * DTB].rearrange("t p (k c) -> p t k c", k=KD))\
                    .then_inc(ublk_in[b % 2], 16)

            sp.dma_start(wq_stage, W_q.rearrange("(g n) c -> n g c", n=HALF)).then_inc(wq_in, 16)
            sp.dma_start(key_stage, keysT).then_inc(wq_in, 16)
            load_u_block(0)
            sp.wait_ge(keyw_mm, 4)
            load_u_block(1)
            for b in range(2, NT // DTB):
                sp.wait_ge(dt_mm, b - 1)
                load_u_block(b)
            sp.dma_start(ut[:, :], uT[0]).then_inc(ut_in, 16)
            sp.wait_ge(z_mm, 2)
            sp.dma_start(ut[:, :], u[0]).then_inc(utok_in, 16)

            def load_u(i):
                sp.wait_ge(bn_ok, 4 * i - 3)
                sp.sem_inc(sp_fence, 1)
                sp.dma_start(ut[:, :], uT[bass.ds(i, 1)].rearrange("t p c -> p (t c)")).then_inc(ut_in, 16)
                sp.wait_ge(z_mm, 2 * i + 2)
                sp.sem_inc(sp_fence, 1)
                sp.dma_start(ut[:, :], u[bass.ds(i, 1)].rearrange("t p c -> p (t c)")).then_inc(utok_in, 16)

            def store(t):
                sp.wait_ge(o_ok, t + 1)
                sp.sem_inc(sp_fence, 1)
                sp.dma_start(out[bass.ds(t, 1)].rearrange("t p c -> p (t c)"), obuf).then_inc(out_done, 16)

            load_u(1)
            with sp.Fori(2, NT) as i:
                load_u(i)
                store(i - 2)
                sp.sem_inc(sp_fence, 1)
            store(NT - 2)
            store(NT - 1)
            sp.wait_ge(out_done, 16 * NT + 16)

        @block.gpsimd
        def _(pool):
            pool.memset(epsc[:, :], EPS).then_inc(zeroed, 1)
            pool.memset(smb[:, :], 0.0).then_inc(out_done, 16)
            pool.memset(state[:, :], 0.0).then_inc(zeroed, 1)
            pool.memset(raw[:, :, 0:TAPS - 1], 0.0).then_inc(zeroed, 1)

            def gathers(t):
                pool.wait_ge(idx_ok, t + 1)
                pool.sem_inc(pool_fence, 1)
                for k in range(PICKS):
                    if k >= RING:
                        if k - RING in PE_ROWS:
                            pool.wait_ge(row_pe, len(PE_ROWS) * t + PE_ROWS.index(k - RING) + 1)
                        else:
                            pool.wait_ge(row_used, len(DVE_ROWS) * t + DVE_ROWS.index(k - RING) + 1)
                        pool.sem_inc(pool_fence, 1)
                    pool.indirect_dma_start(
                        out=ring[:, k % RING, :], out_offset=None, in_=embed,
                        in_offset=bass.IndirectOffsetOnAxis(ap=idx[:, k:k + 1], axis=0))\
                        .then_inc(row_in[k % RING], 16)

            gathers(0)
            with pool.Fori(1, NT) as t:
                gathers(t)

        @block.tensor
        def _(pe):
            pe.wait_ge(wq_in, 32)
            for c in range(KP):
                for b in range(2):
                    for g in range(8):
                        gg = b * 8 + g
                        m = pe.matmul(bank[2 * c + b][:, g * NK:(g + 1) * NK], wq_stage[:, gg, c * P:(c + 1) * P],
                                      key_stage[:, gg, :], start=True, stop=True)
                    m.then_inc(keyw_mm, 1)
            pe.wait_ge(wdt_in, 16)
            for b in range(NT // DTB):
                pe.wait_ge(ublk_in[b % 2], 16 * (b // 2 + 1))
                for j in range(DTB):
                    for k in range(KD):
                        m = pe.matmul(bank[4 + b][:, j * NH:(j + 1) * NH], u_stage[b % 2][:, j, k, :],
                                      w_in[:, k, DPROJ - NH:DPROJ], start=(k == 0), stop=(k == KD - 1))
                m.then_inc(dt_mm, 1)
            pe.wait_ge(w_small, 160)
            pe.wait_ge(keyw_out, 4)
            pe.wait_ge(dt_raw, NT // DTB)
            pe.wait_ge(w_in_in, 16)

            def xbc_proj(i, first):
                pe.wait_ge(ut_in, 16 * i + 16)
                if not first:
                    pe.wait_ge(h1_ok, KU * i)
                    pe.wait_ge(h_ok, i)
                    pe.wait_ge(x1T_ok, i)
                for c in range(KC):
                    for k in range(KD):
                        m = pe.matmul(bank[c // 4][:, (c % 4) * P:(c % 4 + 1) * P],
                                      w_in[:, k, DI + c * P:DI + (c + 1) * P], uT_v[:, k, :],
                                      start=(k == 0), stop=(k == KD - 1))
                    if c in (3, 7, KC - 1):
                        m.then_inc(xbc_mm, 1)

            def z_proj(i, first):
                if not first:
                    pe.wait_ge(hT_ok, i)
                for b in range(2):
                    for k in range(KD):
                        m = pe.matmul(bank[3 + b][:, :], uT_v[:, k, :], w_in[:, k, b * BANK:(b + 1) * BANK],
                                      start=(k == 0), stop=(k == KD - 1))
                    m.then_inc(z_mm, 1)

            def segments(i, first):
                if not first:
                    pe.wait_ge(top1_ok, 3 * i)
                for b, at in enumerate(SEG_BANKS):
                    pe.wait_ge(am_ok, 4 * i + b + 1)
                    if at < 3:
                        pe.wait_ge(tap_ok, KC * i + min(4 * at + 4, KC))
                    pe.matmul(bank[at][:, :], later, seg[:, 4 * b:4 * b + 4, :],
                              start=True, stop=True).then_inc(seg_mm, 1)

            def weighted(t, s):
                for k in PE_ROWS:
                    if k // TOP == s:
                        n = PE_ROWS.index(k)
                        pe.wait_ge(diag_ok, len(PE_ROWS) * t + n + 1)
                        pe.matmul(bank[SUM][:, :], diag_c[:, n % DIAGS, :], ring[:, k % RING, DP:ROW],
                                  start=(n == 0), stop=(n == len(PE_ROWS) - 1)).then_inc(row_pe, 1)

            def tile(i, first, back, ahead):
                def share(s):
                    if back:
                        weighted(i - 1, s)

                pe.wait_ge(xc_ok, i + 1)
                pe.wait_ge(z_ok, 2 * i + 2)
                for c in range(KX):
                    m = pe.transpose(bank[(7, 4)[c // 4]][:, (c % 4) * P:(c % 4 + 1) * P], xc[:, c, :], ident)
                    if c % 4 == 3:
                        m.then_inc(xT_mm, 1)
                pe.transpose(bank[3][:, 0:P], xc[:, KX, :], ident)
                pe.matmul(bank[3][:, P:2 * P], xc[:, KX, :], xc[:, KX + 1, :], start=True, stop=True)
                pe.matmul(bank[3][:, 2 * P:2 * P + NH], upto, cur[:, 1, :], start=True, stop=True)
                pe.matmul(bank[3][:, 3 * P:3 * P + NH], ones, cur[:, 1, :], start=True, stop=True)\
                    .then_inc(cb_mm, 1)
                if first:
                    pe.wait_ge(zeroed, 3)
                else:
                    pe.wait_ge(st_ok, 2 * i)
                pe.wait_ge(e_ok, 4 * i + 3)
                for b in range(2):
                    pe.matmul(bank[b][:, :], xc[:, KX + 1, :], state[:, b * BANK:(b + 1) * BANK],
                              start=True, stop=True).then_inc(yoff_mm, 1)
                share(0)
                if first:
                    pe.wait_ge(const_made, KX)
                pe.wait_ge(xdt_ok, 2 * i + 2)
                pe.wait_ge(g_ok, i + 1)
                for c in range(KX):
                    at = bank[(6, 2)[c // 4]]
                    col = (c % 4) * P
                    pe.matmul(at[:, col:col + P], xc[:, c, :], diag_d[:, c, :], start=(c % 4 == 0), stop=False,
                              skip_group_check=True)
                    for hh in (2 * c, 2 * c + 1):
                        m = pe.matmul(at[:, col + hh % 2 * HD:col + hh % 2 * HD + HD], seg[:, hh, :],
                                      xdt[:, hh * HD:(hh + 1) * HD], start=False,
                                      stop=(c % 4 == 3 and hh % 2 == 1), skip_group_check=True)
                    if c % 4 == 3:
                        m.then_inc(y_mm, 1)
                pe.wait_ge(xdec_ok, i + 1)
                pe.wait_ge(dec_ok, 3 * i + 3)
                for b in range(2):
                    pe.matmul(bank[(7, 4)[b]][:, :], btok, xdec[:, b * BANK:(b + 1) * BANK],
                              start=True, stop=True).then_inc(st_mm, 1)
                share(1)
                pe.wait_ge(y_ok, 2 * i + 2)
                for c in range(KX):
                    m = pe.transpose(bank[(3, 0)[c // 4]][:, (c % 4) * P:(c % 4 + 1) * P], y[:, c * P:(c + 1) * P], ident)
                    if c % 4 == 3:
                        m.then_inc(yT_mm, 1)
                if first:
                    pe.wait_ge(const_made, 2 * KX)
                for c in range(KX):
                    if c % 4 == 0:
                        pe.wait_ge(yT_ok, 2 * i + c // 4 + 1)
                    m = pe.matmul(bank[1][:, :], yT[:, c * P:(c + 1) * P], w_out[:, c, :],
                                  start=(c == 0), stop=(c == KX - 1))
                m.then_inc(op_mm, 1)
                share(2)
                pe.wait_ge(x1_ok, i + 1)
                for k in range(KD):
                    m = pe.transpose(bank[2][:, k * P:(k + 1) * P], x1[:, k * P:(k + 1) * P], ident)
                m.then_inc(x1T_mm, 1)
                share(3)
                if first:
                    pe.wait_ge(w_up_in, 16)
                pe.wait_ge(x1T_ok, i + 1)
                pe.wait_ge(st_ok, 2 * i + 2)
                for c in range(KU):
                    for k in range(KD):
                        m = pe.matmul(bank[UP_BANKS[c // 4]][:, (c % 4) * P:(c % 4 + 1) * P],
                                      w_up[:, k, c * P:(c + 1) * P], x1T[:, k, :], start=(k == 0), stop=(k == KD - 1))
                    if c % 4 == 3:
                        m.then_inc(h1_mm, 1)
                    if c == 7:
                        share(4)
                if first:
                    pe.wait_ge(w_down_in, 16)
                for c in range(KU):
                    if c % 4 == 0:
                        pe.wait_ge(h1_ok, KU * i + c + 4)
                    m = pe.matmul(bank[1][:, 0:DP], h1T[:, c, :], w_down[:, c, :],
                                  start=(c == 0), stop=(c == KU - 1))
                m.then_inc(hp_mm, 1)
                share(5)
                pe.wait_ge(h_ok, i + 1)
                for c in range(KP):
                    m = pe.transpose(bank[4][:, c * P:(c + 1) * P], h[:, c * P:(c + 1) * P], ident)
                m.then_inc(hT_mm, 1)
                pe.wait_ge(hT_ok, i + 1)
                for b in range(2):
                    for c in range(KP):
                        m = pe.matmul(bank[6 + b][:, :], hT[:, c, :], w_key[:, c, b * BANK:(b + 1) * BANK],
                                      start=(c == 0), stop=(c == KP - 1))
                m.then_inc(sim_mm, 1)
                share(6)
                if ahead:
                    xbc_proj(i + 1, False)
                share(7)
                if ahead:
                    z_proj(i + 1, False)
                    segments(i + 1, False)

            xbc_proj(0, True)
            z_proj(0, True)
            segments(0, True)
            tile(0, True, False, True)
            with pe.Fori(1, NT - 1) as i:
                tile(i, False, True, True)
            tile(NT - 1, False, True, False)
            for s in range(EH):
                weighted(NT - 1, s)

        @block.scalar
        def _(act):
            w_in_k = W_in.rearrange("(k p) n -> p k n", p=P)
            act.dma_start(w_in[:, :, DPROJ - NH:DPROJ], w_in_k[:, :, DPROJ - NH:DPROJ]).then_inc(wdt_in, 16)
            act.dma_start(small[:, 0, :], dt_bias).then_inc(w_small, 16)
            act.dma_start(small[:, 1, :], A_log).then_inc(w_small, 16)
            act.dma_start(cst[:, :, :], consts).then_inc(w_small, 16)
            act.dma_start(iota[:, :], iota8).then_inc(w_small, 16)
            act.dma_start(taps[:, :, :], conv_w).then_inc(w_small, 16)
            act.dma_start(cbias[:, :], conv_b).then_inc(w_small, 16)
            act.dma_start(dcol[:, :], D_cols).then_inc(w_small, 16)
            act.dma_start(ncol[:, :], norm_cols).then_inc(w_small, 16)
            act.dma_start(bup[:, :], b_up).then_inc(w_small, 16)
            act.dma_start(bdown[:, :], b_down).then_inc(w_small, 16)
            act.dma_start(w_in[:, :, 0:DPROJ - NH], w_in_k[:, :, 0:DPROJ - NH]).then_inc(w_in_in, 16)
            act.wait_ge(dt_mm, NT // DTB)
            act.dma_start(w_out[:, :, :], W_out.rearrange("(k p) n -> p k n", p=P)).then_inc(w_out_in, 16)
            act.dma_start(w_up[:, :, :], W_upT.rearrange("(k p) n -> p k n", p=P)).then_inc(w_up_in, 16)
            act.dma_start(w_down[:, :, :], W_downT.rearrange("(k p) n -> p k n", p=P)).then_inc(w_down_in, 16)
            act.wait_ge(w_small, 160)
            act.activation(small[:, 2, :], small[:, 1, :], ACT.Exp).then_inc(expa_made, 1)
            act.wait_ge(dt_raw, NT // DTB)
            sp_e = acc[:, 0, :]
            act.activation(sp_e, steps[:, :, :].rearrange("p a b -> p (a b)"), ACT.Abs).then_inc(dt_act, 1)
            act.wait_ge(dt_act, 1)
            act.activation(sp_e, sp_e, ACT.Exp, scale=-1.0).then_inc(dt_act, 1)
            act.wait_ge(zeroed, 3)

            def coefs(t, s):
                act.wait_ge(zp_ok, EH * t + s + 1)
                act.activation(coef[:, s * TOP:(s + 1) * TOP], zp[:, s * TOP:(s + 1) * TOP], ACT.Silu)\
                    .then_inc(coef_ok, 1)
                act.wait_ge(coef_ok, EH * t + s + 1)
                for k in PE_ROWS:
                    if k // TOP == s:
                        n = PE_ROWS.index(k)
                        if n >= DIAGS:
                            act.wait_ge(row_pe, len(PE_ROWS) * t + n - DIAGS + 1)
                        act.activation(diag_c[:, n % DIAGS, :], ident, ACT.Copy, scale=coef[:, k:k + 1])\
                            .then_inc(diag_ok, 1)

            def inputs(i, first):
                if not first:
                    act.wait_ge(conv_ok, KC * 3 * i)
                    act.activation(raw[:, :, 0:TAPS - 1], raw[:, :, P:P + TAPS - 1], ACT.Copy).then_inc(hist_ok, 1)
                    act.wait_ge(hist_ok, i)
                    act.wait_ge(y_mm, 2 * i)
                for b in range(3):
                    n = min(4, KC - 4 * b)
                    act.wait_ge(xbc_mm, 3 * i + b + 1)
                    act.activation(raw[:, 4 * b:4 * b + n, TAPS - 1:],
                                   bank[b][:, 0:n * P].rearrange("p (a c) -> p a c", a=n), ACT.Copy).then_inc(raw_ok, 1)
                    for c in range(4 * b, 4 * b + n):
                        act.activation(xc[:, c, :], bank[b][:, (c % 4) * P:(c % 4 + 1) * P], ACT.Identity,
                                       bias=cbias[:, c:c + 1], scale=taps[:, c, TAPS - 1:TAPS]).then_inc(tap_ok, 1)
                act.wait_ge(cur_ok, 2 * i + 2)
                if not first:
                    act.wait_ge(hp_mm, i)
                for hh in range(NH):
                    m = act.activation(seg[:, hh, :], upto, ACT.Copy, scale=cur[:, 1, hh:hh + 1])
                    if hh % 4 == 3:
                        m.then_inc(am_ok, 1)

            def gates(i, first):
                act.wait_ge(conv_ok, KC * 3 * (i + 1))
                act.activation(xc[:, :, :], xc[:, :, :], ACT.Silu).then_inc(xc_ok, 1)
                for b in range(2):
                    act.wait_ge(z_mm, 2 * i + b + 1)
                    if b == 0 and not first:
                        act.wait_ge(sim_mm, i)
                        act.wait_ge(hcur_ok, i)
                    act.activation(zs[:, b * BANK:(b + 1) * BANK], bank[3 + b][:, :], ACT.Silu).then_inc(z_ok, 1)

            def decays(i, first):
                for b, at in enumerate(SEG_BANKS):
                    act.wait_ge(seg_mm, 4 * i + b + 1)
                    act.activation(seg[:, 4 * b:4 * b + 4, :],
                                   bank[at][:, :].rearrange("p (a c) -> p a c", a=4), ACT.Exp).then_inc(e_ok, 1)
                act.wait_ge(cb_mm, i + 1)
                act.activation(decay[:, 0, :], bank[3][:, 2 * P:2 * P + NH], ACT.Exp).then_inc(dec_ok, 1)
                act.activation(decay[:, 1, :], bank[3][:, 3 * P:3 * P + NH], ACT.Exp).then_inc(dec_ok, 1)
                if not first:
                    act.wait_ge(st_mm, 2 * i)
                    act.wait_ge(g_ok, i)
                act.activation(bcb[:, :, :], bank[3][:, 0:2 * P].rearrange("p (a c) -> p a c", a=2), ACT.Copy)\
                    .then_inc(dec_ok, 1)

            def gated_rms(i):
                for b in range(2):
                    act.wait_ge(yT_mm, 2 * i + b + 1)
                    if b == 0:
                        act.wait_ge(st_mm, 2 * i + 2)
                    act.activation(yT[:, b * BANK:(b + 1) * BANK], bank[(3, 0)[b]][:, :], ACT.Copy).then_inc(yT_ok, 1)
                act.activation(y[:, :], y[:, :], ACT.Square, accum_out=sm[:, 0:1])\
                    .then_inc(sq_ok, 1)
                act.wait_ge(sq_ok, i + 1)
                act.activation(sm[:, 1:2], sm[:, 0:1], ACT.Sqrt, scale=1.0 / DI, bias=epsc[:, :]).then_inc(rms_ok, 1)

            def deviation(i):
                act.wait_ge(bn_ok, 4 * i + 3)
                act.activation(sm[:, 3:4], mv[:, 1:2], ACT.Sqrt, bias=epsc[:, :]).then_inc(ln_ok, 1)

            def turn_x1(i):
                act.wait_ge(x1T_mm, i + 1)
                act.activation(x1T, bank[2][:, :].rearrange("p (a c) -> p a c", a=KD), ACT.Copy).then_inc(x1T_ok, 1)

            def up_silu(i, b):
                act.wait_ge(h1_mm, 4 * i + b + 1)
                for c in range(4 * b, 4 * b + 4):
                    act.activation(h1T[:, c, :], bank[UP_BANKS[b]][:, (c % 4) * P:(c % 4 + 1) * P], ACT.Silu,
                                   bias=bup[:, c:c + 1]).then_inc(h1_ok, 1)

            def turn_h(i):
                act.wait_ge(hT_mm, i + 1)
                act.activation(hT, bank[4][:, 0:DP].rearrange("p (a c) -> p a c", a=KP), ACT.Copy).then_inc(hT_ok, 1)

            def soft_exp(i):
                act.wait_ge(soft_ok, 4 * i + 1)
                act.activation(prob[:, :, :], prob[:, :, :], ACT.Exp).then_inc(exp_ok, 1)

            def back_sqrt(t):
                act.wait_ge(sum_ok, 4 * t + 4)
                act.activation(smb[:, 0:1], mvb[:, 1:2], ACT.Sqrt, bias=epsc[:, :]).then_inc(ln2_ok, 1)

            def hand_over(i, first):
                act.wait_ge(h_ok, i + 1)
                if not first:
                    act.wait_ge(dot_ok, PICKS * i)
                act.activation(hcur[:, :], h, ACT.Copy).then_inc(hcur_ok, 1)

            def tile(i, first, back, ahead):
                def share(s):
                    if back:
                        coefs(i - 1, s)

                gates(i, first)
                share(0)
                decays(i, first)
                share(1)
                gated_rms(i)
                share(2)
                deviation(i)
                share(3)
                turn_x1(i)
                share(4)
                up_silu(i, 0)
                up_silu(i, 1)
                share(5)
                up_silu(i, 2)
                up_silu(i, 3)
                share(6)
                turn_h(i)
                share(7)
                hand_over(i, first)
                if back:
                    back_sqrt(i - 1)
                soft_exp(i)
                if ahead:
                    inputs(i + 1, False)

            inputs(0, True)
            tile(0, True, False, True)
            with act.Fori(1, NT - 1) as i:
                tile(i, False, True, True)
            tile(NT - 1, False, True, False)
            for s in range(EH):
                coefs(NT - 1, s)
            back_sqrt(NT - 1)

        @block.vector
        def _(dve):
            for c in range(2 * KP):
                dve.wait_ge(keyw_mm, c + 1)
                dve.tensor_copy(w_key[:, c // 2, (c % 2) * BANK:(c % 2 + 1) * BANK], bank[c][:, :]).then_inc(keyw_out, 1)
            dve.wait_ge(w_small, 160)
            for c in range(KX):
                dve.tensor_scalar(diag_d[:, c, :], ident, dcol[:, c:c + 1], None, ALU.mult).then_inc(const_made, 1)
            sp_x = steps[:, :, :].rearrange("p a b -> p (a b)")
            sp_e, sp_p, sp_r = acc[:, 0, :], acc[:, 1, :], x1[:, :]
            for b in range(NT // DTB):
                dve.wait_ge(dt_mm, b + 1)
                dve.tensor_tensor(steps[:, b * DTB:(b + 1) * DTB, :],
                                  bank[4 + b][:, 0:DTB * NH].rearrange("p (t n) -> p t n", n=NH),
                                  small[:, 0:1, :].to_broadcast([P, DTB, NH]), ALU.add).then_inc(dt_raw, 1)
            dve.wait_ge(dt_act, 2)
            dve.tensor_scalar(sp_r, sp_e, 2.0, None, ALU.add).then_inc(dt_dve, 1)
            dve.wait_ge(dt_dve, 1)
            dve.reciprocal(sp_r, sp_r).then_inc(dt_dve, 1)
            dve.wait_ge(dt_dve, 2)
            dve.tensor_tensor(sp_r, sp_e, sp_r, ALU.mult).then_inc(dt_dve, 1)
            dve.wait_ge(dt_dve, 3)
            dve.tensor_tensor(sp_e, sp_r, sp_r, ALU.mult).then_inc(dt_dve, 1)
            dve.wait_ge(dt_dve, 4)
            dve.tensor_scalar(sp_p, sp_e, 1.0 / 17, None, ALU.mult).then_inc(dt_dve, 1)
            for n, odd in enumerate((15, 13, 11, 9, 7, 5, 3)):
                dve.wait_ge(dt_dve, 5 + n)
                dve.scalar_tensor_tensor(out=sp_p, in0=sp_p, scalar=1.0 / odd, in1=sp_e, op0=ALU.add, op1=ALU.mult)\
                    .then_inc(dt_dve, 1)
            dve.wait_ge(dt_dve, 12)
            dve.scalar_tensor_tensor(out=sp_p, in0=sp_p, scalar=1.0, in1=sp_r, op0=ALU.add, op1=ALU.mult)\
                .then_inc(dt_dve, 1)
            dve.tensor_scalar(sp_x, sp_x, 0.0, 0.5, ALU.max, ALU.mult).then_inc(dt_dve, 1)
            dve.wait_ge(dt_dve, 14)
            dve.tensor_tensor(sp_p, sp_p, sp_x, ALU.add).then_inc(dt_dve, 1)
            dve.wait_ge(dt_dve, 15)
            dve.tensor_scalar(sp_x, sp_p, 2.0, None, ALU.mult).then_inc(dt_dve, 1)
            dve.wait_ge(dt_dve, 16)
            dve.wait_ge(expa_made, 1)
            dve.wait_ge(zeroed, 3)

            def heads(ap):
                return ap.rearrange("p (n c) -> p n c", c=HD)

            def time_steps(i):
                dt_i = steps[:, bass.ds(i, 1), :]
                dve.tensor_scalar(cur[:, 0:1, :], dt_i, 1.0, None, ALU.mult).then_inc(cur_ok, 1)
                dve.scalar_tensor_tensor(out=cur[:, 1:2, :], in0=dt_i, scalar=-1.0, in1=small[:, 2:3, :],
                                         op0=ALU.mult, op1=ALU.mult).then_inc(cur_ok, 1)

            def convolve(i):
                for j in range(TAPS - 1):
                    for c in range(KC):
                        if j == 0:
                            dve.wait_ge(tap_ok, KC * i + c + 1)
                        else:
                            dve.wait_ge(conv_ok, KC * (3 * i + j - 1) + c + 1)
                        dve.scalar_tensor_tensor(out=xc[:, c, :], in0=raw[:, c, j:j + P], scalar=taps[:, c, j:j + 1],
                                                 in1=xc[:, c, :], op0=ALU.mult, op1=ALU.add).then_inc(conv_ok, 1)

            def scan_in(i, first):
                if not first:
                    dve.wait_ge(out_done, 16 * i)
                for b in range(2):
                    dve.wait_ge(xT_mm, 2 * i + b + 1)
                    dve.tensor_tensor(heads(xdt[:, b * BANK:(b + 1) * BANK]), heads(bank[(7, 4)[b]][:, :]),
                                      cur[:, 0, 8 * b:8 * b + 8].unsqueeze(2).to_broadcast([P, 8, HD]),
                                      ALU.mult).then_inc(xdt_ok, 1)
                dve.wait_ge(dec_ok, 3 * i + 3)
                dve.tensor_tensor(cbm, cbm, upto, ALU.mult).then_inc(cbm_ok, 1)
                dve.wait_ge(xdt_ok, 2 * i + 2)
                dve.wait_ge(e_ok, 4 * i + 4)
                dve.tensor_tensor(heads(xdec[:, :]), heads(xdt[:, :]),
                                  seg[:, :, P - 1:P].to_broadcast([P, NH, HD]), ALU.mult).then_inc(xdec_ok, 1)
                dve.wait_ge(cbm_ok, i + 1)
                dve.wait_ge(xdec_ok, i + 1)
                dve.tensor_tensor(seg[:, :, :], seg[:, :, :], cbm.unsqueeze(1).to_broadcast([P, NH, P]),
                                  ALU.mult).then_inc(g_ok, 1)

            def scan_out(i):
                dve.wait_ge(yoff_mm, 2 * i + 2)
                dve.tensor_tensor(heads(state[:, :]), heads(state[:, :]),
                                  decay[:, 1, :].unsqueeze(2).to_broadcast([P, NH, HD]), ALU.mult).then_inc(dcy_ok, 1)
                for b in range(2):
                    dve.wait_ge(y_mm, 2 * i + 2)
                    dve.tensor_tensor(heads(y[:, b * BANK:(b + 1) * BANK]), heads(bank[b][:, :]),
                                      decay[:, 0, 8 * b:8 * b + 8].unsqueeze(2).to_broadcast([P, 8, HD]),
                                      ALU.mult).then_inc(yoff_ok, 1)
                for b in range(2):
                    dve.wait_ge(yoff_ok, 2 * i + b + 1)
                    dve.tensor_tensor(y[:, b * BANK:(b + 1) * BANK], y[:, b * BANK:(b + 1) * BANK], bank[(6, 2)[b]][:, :],
                                      ALU.add).then_inc(y_half, 1)
                dve.wait_ge(z_ok, 2 * i + 2)
                for b in range(2):
                    dve.wait_ge(y_half, 2 * i + b + 1)
                    dve.tensor_tensor(y[:, b * BANK:(b + 1) * BANK], y[:, b * BANK:(b + 1) * BANK],
                                      zs[:, b * BANK:(b + 1) * BANK], ALU.mult).then_inc(y_ok, 1)
                dve.wait_ge(dcy_ok, i + 1)
                for b in range(2):
                    dve.wait_ge(st_mm, 2 * i + b + 1)
                    dve.tensor_tensor(state[:, b * BANK:(b + 1) * BANK], state[:, b * BANK:(b + 1) * BANK],
                                      bank[(7, 4)[b]][:, :], ALU.add).then_inc(st_ok, 1)

            def residual(i):
                dve.wait_ge(rms_ok, i + 1)
                dve.reciprocal(sm[:, 2:3], sm[:, 1:2]).then_inc(rr_ok, 1)
                dve.wait_ge(rr_ok, i + 1)
                dve.wait_ge(op_mm, i + 1)
                dve.wait_ge(utok_in, 16 * i + 16)
                dve.scalar_tensor_tensor(out=x1[:, :], in0=bank[1][:, :], scalar=sm[:, 2:3], in1=ut[:, :],
                                         op0=ALU.mult, op1=ALU.add).then_inc(bn_ok, 1)
                dve.wait_ge(bn_ok, 4 * i + 1)
                dve.bn_stats(st6[:, :], x1[:, :]).then_inc(bn_ok, 1)
                dve.wait_ge(bn_ok, 4 * i + 2)
                dve.sem_inc(dve_fence, 1)
                dve.bn_aggr(mv[:, :], st6[:, :]).then_inc(bn_ok, 1)

            def norm1(i):
                dve.wait_ge(ln_ok, i + 1)
                dve.reciprocal(sm[:, 4:5], sm[:, 3:4]).then_inc(bn_ok, 1)
                dve.wait_ge(bn_ok, 4 * i + 4)
                dve.tensor_scalar(x1[:, :], x1[:, :], mv[:, 0:1], sm[:, 4:5], ALU.subtract, ALU.mult).then_inc(x1_ok, 1)

            def private(i):
                dve.wait_ge(hp_mm, i + 1)
                dve.tensor_tensor(h, bank[1][:, 0:DP], bdown[:, :], ALU.add).then_inc(h_ok, 1)

            def top_halves(i):
                dve.wait_ge(sim_mm, i + 1)
                dve.sem_inc(dve_fence, 1)
                for g in range(NG):
                    m = dve.max(out=v1[:, g, :], in_=bank[6 + g // 8][:, (g % 8) * NK:(g % 8 + 1) * NK])
                m.then_inc(top1_ok, 1)
                dve.wait_ge(top1_ok, 3 * i + 1)
                dve.sem_inc(dve_fence, 1)
                for g in range(NG):
                    m = dve.max_index(i1[:, g, :], v1[:, g, :], bank[6 + g // 8][:, (g % 8) * NK:(g % 8 + 1) * NK])
                m.then_inc(top1_ok, 1)
                dve.tensor_tensor(allsc.rearrange("p n (a b) -> p n a b", a=TOP),
                                  v1[:, 0:EH, :].unsqueeze(3).to_broadcast([P, EH, TOP, TOP]),
                                  v1[:, EH:NG, :].unsqueeze(2).to_broadcast([P, EH, TOP, TOP]), ALU.add).then_inc(top1_ok, 1)

            def top_pairs(i):
                dve.wait_ge(top1_ok, 3 * i + 3)
                dve.sem_inc(dve_fence, 1)
                for n in range(EH):
                    m = dve.max(out=v2[:, n, :], in_=allsc[:, n, :])
                m.then_inc(top2_ok, 1)
                dve.wait_ge(top2_ok, 4 * i + 1)
                dve.sem_inc(dve_fence, 1)
                for n in range(EH):
                    m = dve.max_index(pk[:, n, :], v2[:, n, :], allsc[:, n, :])
                m.then_inc(top2_ok, 1)
                dve.tensor_tensor(prob[:, :, :], v2[:, :, :], v2[:, :, 0:1].to_broadcast([P, EH, TOP]), ALU.subtract)\
                    .then_inc(soft_ok, 1)
                dve.wait_ge(top2_ok, 4 * i + 2)
                pk_v = pk[:, :, :].rearrange("p a b -> p (a b)")
                dve.tensor_scalar(ak[:, :], pk_v, 3, None, ALU.logical_shift_right).then_inc(top2_ok, 1)
                dve.tensor_scalar(bk[:, :], pk_v, TOP - 1, None, ALU.bitwise_and).then_inc(top2_ok, 1)
                hot_x = allsc.rearrange("p n (k a) -> p n k a", a=TOP)
                hot_y = hot.rearrange("p (n k) a -> p n k a", n=EH)
                for n, (place, one) in enumerate(((ak, hot_x), (bk, hot_y))):
                    dve.wait_ge(top2_ok, 4 * i + 3 + n)
                    dve.tensor_tensor(one.rearrange("p n k a -> p (n k) a"),
                                      place[:, :].unsqueeze(2).to_broadcast([P, PICKS, TOP]),
                                      iota[:, :].unsqueeze(1).to_broadcast([P, PICKS, TOP]),
                                      ALU.is_equal).then_inc(hot_ok, 1)
                for n, one in enumerate((hot_x, hot_y)):
                    dve.wait_ge(hot_ok, 2 * i + n + 1)
                    dve.tensor_tensor(one, one, i1[:, n * EH:(n + 1) * EH, :].unsqueeze(2).to_broadcast([P, EH, TOP, TOP]),
                                      ALU.mult).then_inc(pick_ok, 1)
                for n, one in enumerate((hot_x, hot_y)):
                    dve.wait_ge(pick_ok, 2 * i + n + 1)
                    dve.tensor_reduce(ixy[:, n, :], one.rearrange("p n k a -> p (n k) a"), AX.X, ALU.add).then_inc(ixy_ok, 1)
                dve.wait_ge(ixy_ok, 2 * i + 2)
                dve.scalar_tensor_tensor(out=idx[:, :], in0=ixy[:, 0, :], scalar=float(NK), in1=ixy[:, 1, :],
                                         op0=ALU.mult, op1=ALU.add).then_inc(idx_ok, 1)

            def softmax(i):
                dve.wait_ge(exp_ok, i + 1)
                dve.tensor_reduce(psm[:, 0, :], prob[:, :, :], AX.X, ALU.add).then_inc(soft_ok, 1)
                dve.wait_ge(soft_ok, 4 * i + 2)
                dve.reciprocal(psm[:, 1, :], psm[:, 0, :]).then_inc(soft_ok, 1)
                dve.wait_ge(soft_ok, 4 * i + 3)
                dve.tensor_tensor(prob[:, :, :], prob[:, :, :], psm[:, 1, :].unsqueeze(2).to_broadcast([P, EH, TOP]),
                                  ALU.mult).then_inc(soft_ok, 1)

            def experts(t, s):
                if s == 0:
                    dve.wait_ge(hcur_ok, t + 1)
                for k in range(s * TOP, (s + 1) * TOP):
                    uses = len(range(k % RING, PICKS, RING))
                    dve.wait_ge(row_in[k % RING], 16 * (uses * t + k // RING + 1))
                    dve.scalar_tensor_tensor(out=ring[:, k % RING, 0:DP], in0=ring[:, k % RING, 0:DP], scalar=1.0,
                                             in1=hcur[:, :], op0=ALU.mult, op1=ALU.mult,
                                             accum_out=dots[:, k:k + 1]).then_inc(dot_ok, 1)
                dve.wait_ge(dot_ok, PICKS * t + (s + 1) * TOP)
                if s == 0:
                    dve.wait_ge(soft_ok, 4 * t + 4)
                dve.tensor_tensor(zp[:, s * TOP:(s + 1) * TOP], dots[:, s * TOP:(s + 1) * TOP], prob[:, s, :], ALU.mult)\
                    .then_inc(zp_ok, 1)
                dve.wait_ge(coef_ok, EH * t + s + 1)
                for k in DVE_ROWS:
                    if k // TOP != s:
                        continue
                    n = DVE_ROWS.index(k)
                    if n >= 2:
                        dve.wait_ge(row_used, len(DVE_ROWS) * t + n - 1)
                    if n == 1:
                        dve.tensor_scalar(acc[:, 1, :], ring[:, k % RING, DP:ROW], coef[:, k:k + 1], None, ALU.mult)\
                            .then_inc(row_used, 1)
                    else:
                        dve.scalar_tensor_tensor(out=acc[:, n % 2, :], in0=ring[:, k % RING, DP:ROW],
                                                 scalar=coef[:, k:k + 1], in1=x1[:, :] if n == 0 else acc[:, n % 2, :],
                                                 op0=ALU.mult, op1=ALU.add).then_inc(row_used, 1)

            def back_stats(t):
                dve.wait_ge(row_used, len(DVE_ROWS) * (t + 1))
                dve.tensor_tensor(acc[:, 0, :], acc[:, 0, :], acc[:, 1, :], ALU.add).then_inc(sum_ok, 1)
                dve.wait_ge(sum_ok, 4 * t + 1)
                dve.wait_ge(row_pe, len(PE_ROWS) * (t + 1))
                dve.tensor_tensor(acc[:, 0, :], acc[:, 0, :], bank[SUM][:, :], ALU.add).then_inc(sum_ok, 1)
                dve.wait_ge(sum_ok, 4 * t + 2)
                dve.bn_stats(st6b[:, :], acc[:, 0, :]).then_inc(sum_ok, 1)
                dve.wait_ge(sum_ok, 4 * t + 3)
                dve.sem_inc(dve_fence, 1)
                dve.bn_aggr(mvb[:, :], st6b[:, :]).then_inc(sum_ok, 1)

            def back_norm(t):
                dve.wait_ge(ln2_ok, t + 1)
                dve.reciprocal(smb[:, 1:2], smb[:, 0:1]).then_inc(r2_ok, 1)
                dve.wait_ge(r2_ok, t + 1)
                dve.tensor_scalar(obuf, acc[:, 0, :], mvb[:, 0:1], smb[:, 1:2], ALU.subtract, ALU.mult)\
                    .then_inc(o_ok, 1)

            def tile(i, first, back, ahead):
                def share(s):
                    if back:
                        experts(i - 1, s)

                share(0)
                scan_in(i, first)
                share(1)
                scan_out(i)
                share(2)
                residual(i)
                share(3)
                norm1(i)
                share(4)
                share(5)
                private(i)
                share(6)
                top_halves(i)
                share(7)
                if back:
                    back_stats(i - 1)
                if ahead:
                    time_steps(i + 1)
                top_pairs(i)
                softmax(i)
                if back:
                    back_norm(i - 1)
                if ahead:
                    convolve(i + 1)

            time_steps(0)
            convolve(0)
            dve.wait_ge(w_out_in, 16)
            for c in range(KX):
                dve.tensor_scalar(w_out[:, c, :], w_out[:, c, :], ncol[:, c:c + 1], None, ALU.mult)\
                    .then_inc(const_made, 1)
            tile(0, True, False, True)
            with dve.Fori(1, NT - 1) as i:
                tile(i, False, True, True)
            tile(NT - 1, False, True, False)
            for s in range(EH):
                experts(NT - 1, s)
            back_stats(NT - 1)
            dve.wait_ge(out_done, 16 * NT)
            back_norm(NT - 1)


def kernel(L0_attn_u, L0_attn_W_in, L0_attn_conv_w, L0_attn_conv_b, L0_attn_dt_bias, L0_attn_A_log, L0_attn_D,
           L0_attn_norm_scale, L0_attn_W_out, L0_ffn_W_up, L0_ffn_b_up, L0_ffn_W_down, L0_ffn_b_down,
           L0_ffn_W_q, L0_ffn_keys, L0_ffn_down_embed, L0_ffn_up_embed):
    import concourse.bacc as bacc
    from concourse.bass_utils import run_bass_kernel_spmd

    def a(x):
        return np.asarray(x)

    def c(x):
        return np.ascontiguousarray(x)

    def rows(x):
        return c(np.broadcast_to(a(x)[None, :], (P, x.shape[0])))

    def cols(x, n):
        return c(a(x).reshape(n, P).T)

    u = a(L0_attn_u).reshape(NT, P, D)
    q = np.arange(P)
    consts = np.stack([q[:, None] == q[None, :], q[:, None] > q[None, :], q[:, None] <= q[None, :],
                       q[:, None] >= 0 * q[None, :]], 1).astype(np.float32)
    arrays = {
        "uT": c(u.reshape(NT, P, KD, P).transpose(0, 3, 2, 1).reshape(NT, P, D)),
        "u": c(u),
        "W_in": c(a(L0_attn_W_in)),
        "W_out": c(a(L0_attn_W_out)),
        "W_upT": c(a(L0_ffn_W_up).T),
        "W_downT": c(a(L0_ffn_W_down).T),
        "W_q": c(a(L0_ffn_W_q)),
        "keysT": c(a(L0_ffn_keys).transpose(3, 2, 0, 1).reshape(HALF, NG, NK)),
        "embed": c(np.concatenate([a(L0_ffn_down_embed), a(L0_ffn_up_embed)], 1)),
        "consts": consts,
        "iota8": c(np.broadcast_to(np.arange(TOP, dtype=np.float32), (P, TOP))),
        "conv_w": c(a(L0_attn_conv_w).reshape(TAPS, KC, P).transpose(2, 1, 0)),
        "conv_b": cols(L0_attn_conv_b, KC),
        "dt_bias": rows(L0_attn_dt_bias),
        "A_log": rows(L0_attn_A_log),
        "D_cols": cols(np.repeat(a(L0_attn_D), HD), KX),
        "norm_cols": cols(L0_attn_norm_scale, KX),
        "b_up": cols(L0_ffn_b_up, KU),
        "b_down": rows(L0_ffn_b_down),
    }
    nc = bacc.Bacc("TRN2", target_bir_lowering=False, num_devices=1)
    args = [nc.dram_tensor(n, x.shape, mybir.dt.from_np(x.dtype), kind="ExternalInput").ap() for n, x in arrays.items()]
    args.append(nc.dram_tensor("out", (NT, P, D), F32, kind="ExternalOutput").ap())
    build(nc, *args)
    r = run_bass_kernel_spmd(nc, [arrays], core_ids=[0])
    return r.results[0]["out"].reshape(1, T, D)
```

```python
from contextlib import ExitStack

import numpy as np

import concourse.bass as bass
from concourse import mybir

F32 = mybir.dt.float32
U32 = mybir.dt.uint32
ALU = mybir.AluOpType
ACT = mybir.ActivationFunctionType
AX = mybir.AxisListType

P = 128
T = 4096
D = 512
DI = 1024
NS = 128
NH = 16
HD = 64
TAPS = 4
CONV = DI + 2 * NS
DPROJ = 2 * DI + 2 * NS + NH
DC = 2048
DP = 256
EH = 8
TOP = 8
NK = 64
HALF = 64
NE = NK * NK
ROW = DP + D
NT = T // P
KD = D // P
KC = CONV // P
KX = DI // P
KU = DC // P
KP = DP // P
RING = 13
PICKS = EH * TOP
NG = 2 * EH
DTB = 8
EPS = 1e-5
BANK = 512
DIAGS = 3
GROUP = 4
STEPS = PICKS // GROUP
ON_PE = (1, 1, 1, 1, 1, 2, 3, 2, 2, 2, 2, 1, 1, 1, 0, 0)
EARLY = (4, 6, 9)
FIRST_ODD = 3
PE_ROWS = [k for k in range(PICKS) if k % GROUP >= GROUP - ON_PE[k // GROUP]]
DVE_ROWS = [k for k in range(PICKS) if k not in PE_ROWS]


def build(nc, uT, u, W_in, W_out, W_upT, W_downT, W_q, keysT, embed, consts, iota8, conv_w, conv_b,
          dt_bias, A_log, D_cols, norm_cols, b_up, b_down, out):
    with ExitStack() as ctx:
        def sb(name, shape, dt=F32):
            return ctx.enter_context(nc.sbuf_tensor(name, shape, dt))

        def sem(name):
            return ctx.enter_context(nc.semaphore(name))

        w_in = sb("w_in", [P, KD, DPROJ])
        w_out = sb("w_out", [P, KX, D])
        w_up = sb("w_up", [P, KD, DC])
        w_down = sb("w_down", [P, KU, DP])
        w_key = sb("w_key", [P, KP, NG * NK])
        cst = sb("cst", [P, 4, P])
        ident, later, upto, ones = (cst[:, n, :] for n in range(4))
        diag_d = sb("diag_d", [P, KX, P])
        iota = sb("iota", [P, TOP])
        taps = sb("taps", [P, KC, TAPS])
        cbias = sb("cbias", [P, KC])
        dcol = sb("dcol", [P, KX])
        ncol = sb("ncol", [P, KX])
        bup = sb("bup", [P, KU])
        bdown = sb("bdown", [P, DP])
        small = sb("small", [P, 3, NH])
        steps = sb("steps", [P, NT, NH])
        epsc = sb("epsc", [P, 1])
        ring = sb("ring", [P, RING, ROW])
        ut = sb("ut", [P, D])
        h = sb("h", [P, DP])
        raw = sb("raw", [P, KC, TAPS - 1 + P])
        xc = sb("xc", [P, KC, P])
        zs = sb("zs", [P, DI])
        cur = sb("cur", [P, 2, NH])
        decay = sb("decay", [P, 3, NH])
        seg = sb("seg", [P, NH, P])
        bcb = sb("bcb", [P, 2, P])
        xdt = sb("xdt", [P, DI])
        xdec = sb("xdec", [P, DI])
        state = sb("state", [P, DI])
        x1 = sb("x1", [P, D])
        st6 = sb("st6", [P, 6])
        mv = sb("mv", [P, 2])
        sm = sb("sm", [P, 8])
        v1 = sb("v1", [P, NG, TOP])
        i1 = sb("i1", [P, NG, TOP], U32)
        v2 = sb("v2", [P, EH, TOP])
        pk = sb("pk", [P, EH, TOP], U32)
        bk = sb("bk", [P, PICKS], U32)
        ixy = sb("ixy", [P, 2, PICKS])
        idx = sb("idx", [P, 2, PICKS], U32)
        prob = sb("prob", [P, EH, TOP])
        psm = sb("psm", [P, 2, EH])
        hcur = sb("hcur", [P, DP])
        acc = sb("acc", [P, 2, D])
        dots = sb("dots", [P, PICKS])
        zp = sb("zp", [P, PICKS])
        coef = sb("coef", [P, PICKS])
        diag_c = sb("diag_c", [P, DIAGS, P])
        st6b = sb("st6b", [P, 6])
        mvb = sb("mvb", [P, 2])
        smb = sb("smb", [P, 2])

        uT_v = ut[:, :].rearrange("p (k c) -> p k c", k=KD)
        btok, cbm = bcb[:, 0, :], bcb[:, 1, :]
        y = xdt
        yT = xdec
        h1T = seg
        u_tok = zs[:, D:DI]
        x1T = zs[:, 0:D].rearrange("p (k c) -> p k c", k=KD)
        hT = zs[:, D + DP:DI].rearrange("p (k c) -> p k c", k=KP)
        allsc = xdt[:, 0:BANK].rearrange("p (n c) -> p n c", n=EH)
        hot = xdt[:, BANK:DI].rearrange("p (k c) -> p k c", k=PICKS)
        raised = ixy[:, 0, :].rearrange("p (n k) -> p n k", k=TOP)
        x1_new = xdt[:, 0:D]
        obuf = acc[:, 1, :]
        bank = [ctx.enter_context(nc.psum_tensor(f"bank{n}", [P, BANK], F32)) for n in range(8)]
        Z_BANKS, SEG_BANKS, XT_BANKS, MISC, YOFF_BANKS = (0, 2), (4, 1, 3, 0), (1, 3), 2, (4, 0)
        Y_BANKS, ST_BANKS, YT_BANKS, OP, XBC_BANKS = (6, 7), (1, 3), (2, 4), 0, (6, 7, 1)
        X1T, UP_BANKS, DOWN, HT, SIM_BANKS, SUM = 3, (2, 4, 0, 6), 7, 1, (6, 7), 5

        stage = ring[:, :, :].rearrange("p a b -> p (a b)")
        WQ_END = NG * DP + NG * NK
        wq_stage = stage[0:HALF, 0:NG * DP].rearrange("p (g c) -> p g c", g=NG)
        key_stage = stage[0:HALF, NG * DP:WQ_END].rearrange("p (g c) -> p g c", g=NG)
        u_stage = [stage[:, a:a + DTB * D].rearrange("p (t k c) -> p t k c", t=DTB, k=KD) for a in (WQ_END, 0)]

        w_small, wdt_in = sem("w_small"), sem("wdt_in")
        w_in_in, w_out_in, w_up_in, w_down_in, wq_in = (
            sem(n) for n in ("w_in_in", "w_out_in", "w_up_in", "w_down_in", "wq_in"))
        ublk_in, ut_in, utok_in = [sem("ublk_in0"), sem("ublk_in1")], sem("ut_in"), sem("utok_in")
        row_in = [sem(f"row_in{n}") for n in range(RING)]
        out_done = sem("out_done")
        zeroed, const_made, expa_made = sem("zeroed"), sem("const_made"), sem("expa_made")
        keyw_mm, keyw_out = sem("keyw_mm"), sem("keyw_out")
        dt_mm, dt_raw, dt_act, dt_dve = sem("dt_mm"), sem("dt_raw"), sem("dt_act"), sem("dt_dve")
        xbc_mm, z_mm, seg_mm, xT_mm, cb_mm, yoff_mm, y_mm, st_mm = (
            sem(n) for n in ("xbc_mm", "z_mm", "seg_mm", "xT_mm", "cb_mm", "yoff_mm", "y_mm", "st_mm"))
        yT_mm, op_mm, x1T_mm, h1_mm, hp_mm, hT_mm, sim_mm, row_pe = (
            sem(n) for n in ("yT_mm", "op_mm", "x1T_mm", "h1_mm", "hp_mm", "hT_mm", "sim_mm", "row_pe"))
        hist_ok, raw_ok, tap_ok, xc_ok, z_ok, am_ok, e_ok, dec_ok = (
            sem(n) for n in ("hist_ok", "raw_ok", "tap_ok", "xc_ok", "z_ok", "am_ok", "e_ok", "dec_ok"))
        yT_ok, sq_ok, rms_ok, ln_ok, x1T_ok, h1_ok, hT_ok, exp_ok, hcur_ok, coef_ok, diag_ok, ln2_ok, kept_ok, saved_ok, table_in = (
            sem(n) for n in ("yT_ok", "sq_ok", "rms_ok", "ln_ok", "x1T_ok", "h1_ok", "hT_ok", "exp_ok", "hcur_ok",
                             "coef_ok", "diag_ok", "ln2_ok", "kept_ok", "saved_ok", "table_in"))
        cur_ok, conv_ok, cbm_ok, xdt_ok, g_ok, xdec_ok, yoff_ok, y_half, y_ok, dcy_ok, st_ok, rr_ok, bn_ok, x1_ok, h_ok = (
            sem(n) for n in ("cur_ok", "conv_ok", "cbm_ok", "xdt_ok", "g_ok", "xdec_ok", "yoff_ok", "y_half", "y_ok",
                             "dcy_ok", "st_ok", "rr_ok", "bn_ok", "x1_ok", "h_ok"))
        top1_ok, top2_ok, hot_ok, pick_ok, ixy_ok, idx_ok, soft_ok, dot_ok, zp_ok, row_used, sum_ok, r2_ok, o_ok = (
            sem(n) for n in ("top1_ok", "top2_ok", "hot_ok", "pick_ok", "ixy_ok", "idx_ok", "soft_ok", "dot_ok",
                             "zp_ok", "row_used", "sum_ok", "r2_ok", "o_ok"))
        dve_fence, pool_fence, sp_fence = sem("dve_fence"), sem("pool_fence"), sem("sp_fence")

        block = ctx.enter_context(nc.Block())

        @block.sync
        def _(sp):
            def load_u_block(b):
                sp.dma_start(u_stage[b % 2], uT[b * DTB:(b + 1) * DTB].rearrange("t p (k c) -> p t k c", k=KD))\
                    .then_inc(ublk_in[b % 2], 16)

            sp.dma_start(wq_stage, W_q.rearrange("(g n) c -> n g c", n=HALF)).then_inc(wq_in, 16)
            sp.dma_start(key_stage, keysT).then_inc(wq_in, 16)
            load_u_block(0)
            sp.wait_ge(keyw_mm, 4)
            load_u_block(1)
            for b in range(2, NT // DTB):
                sp.wait_ge(dt_mm, b - 1)
                load_u_block(b)
            sp.dma_start(ut[:, :], uT[0]).then_inc(ut_in, 16)
            sp.wait_ge(y_ok, 2)
            sp.dma_start(u_tok, u[0]).then_inc(utok_in, 16)

            def load_ut(i):
                sp.wait_ge(z_mm, 2 * i)
                sp.sem_inc(sp_fence, 1)
                sp.dma_start(ut[:, :], uT[bass.ds(i, 1)].rearrange("t p c -> p (t c)")).then_inc(ut_in, 16)

            def load_u(i):
                sp.wait_ge(y_ok, 2 * i + 2)
                sp.sem_inc(sp_fence, 1)
                sp.dma_start(u_tok, u[bass.ds(i, 1)].rearrange("t p c -> p (t c)")).then_inc(utok_in, 16)

            def store(t):
                sp.wait_ge(o_ok, t + 1)
                sp.sem_inc(sp_fence, 1)
                sp.dma_start(out[bass.ds(t, 1)].rearrange("t p c -> p (t c)"), obuf).then_inc(out_done, 16)

            load_ut(1)
            load_u(1)
            load_ut(2)
            with sp.Fori(2, NT - 1) as i:
                load_u(i)
                load_ut(i + 1)
                store(i - 2)
                sp.sem_inc(sp_fence, 1)
            load_u(NT - 1)
            store(NT - 3)
            store(NT - 2)
            store(NT - 1)
            sp.wait_ge(out_done, 16 * NT + 16)

        @block.gpsimd
        def _(pool):
            pool.memset(epsc[:, :], EPS).then_inc(zeroed, 1)
            pool.memset(smb[:, :], 0.0).then_inc(out_done, 16)
            pool.memset(state[:, :], 0.0).then_inc(zeroed, 1)
            pool.memset(raw[:, :, 0:TAPS - 1], 0.0).then_inc(zeroed, 1)

            def gathers(t, half, first):
                pool.wait_ge(idx_ok, t + 1)
                pool.sem_inc(pool_fence, 1)
                for k in range(PICKS):
                    j, of = (k - RING, t) if k >= RING else (max(range(k, PICKS, RING)), t - 1)
                    if k >= RING or not first:
                        if j in PE_ROWS:
                            pool.wait_ge(row_pe, len(PE_ROWS) * of + PE_ROWS.index(j) + 1)
                        else:
                            pool.wait_ge(row_used, len(DVE_ROWS) * of + DVE_ROWS.index(j) + 1)
                        pool.sem_inc(pool_fence, 1)
                    pool.indirect_dma_start(
                        out=ring[:, k % RING, :], out_offset=None, in_=embed,
                        in_offset=bass.IndirectOffsetOnAxis(ap=idx[:, half, k:k + 1], axis=0))\
                        .then_inc(row_in[k % RING], 16)

            gathers(0, 0, True)
            with pool.Fori(0, (NT - 2) // 2) as j:
                gathers(2 * j + 1, 1, False)
                gathers(2 * j + 2, 0, False)
            gathers(NT - 1, 1, False)

        @block.tensor
        def _(pe):
            pe.wait_ge(wq_in, 32)
            for c in range(KP):
                for b in range(2):
                    for g in range(8):
                        gg = b * 8 + g
                        m = pe.matmul(bank[2 * c + b][:, g * NK:(g + 1) * NK], wq_stage[:, gg, c * P:(c + 1) * P],
                                      key_stage[:, gg, :], start=True, stop=True)
                    m.then_inc(keyw_mm, 1)
            pe.wait_ge(wdt_in, 16)
            for b in range(NT // DTB):
                pe.wait_ge(ublk_in[b % 2], 16 * (b // 2 + 1))
                for j in range(DTB):
                    for k in range(KD):
                        m = pe.matmul(bank[4 + b][:, j * NH:(j + 1) * NH], u_stage[b % 2][:, j, k, :],
                                      w_in[:, k, DPROJ - NH:DPROJ], start=(k == 0), stop=(k == KD - 1))
                m.then_inc(dt_mm, 1)
            pe.wait_ge(w_small, 160)
            pe.wait_ge(keyw_out, 4)
            pe.wait_ge(dt_raw, NT // DTB)
            pe.wait_ge(w_in_in, 16)

            def xbc_proj(i, first):
                pe.wait_ge(ut_in, 16 * i + 16)
                if not first:
                    pe.wait_ge(y_ok, 2 * i)
                    pe.wait_ge(st_ok, 2 * i - 1)
                for c in range(KC):
                    for k in range(KD):
                        m = pe.matmul(bank[XBC_BANKS[c // 4]][:, (c % 4) * P:(c % 4 + 1) * P],
                                      w_in[:, k, DI + c * P:DI + (c + 1) * P], uT_v[:, k, :],
                                      start=(k == 0), stop=(k == KD - 1))
                    if c in (3, 7, KC - 1):
                        m.then_inc(xbc_mm, 1)

            def lead(i, first, share):
                for b in range(2):
                    for k in range(KD):
                        m = pe.matmul(bank[Z_BANKS[b]][:, :], uT_v[:, k, :], w_in[:, k, b * BANK:(b + 1) * BANK],
                                      start=(k == 0), stop=(k == KD - 1))
                    m.then_inc(z_mm, 1)
                    if b == 0:
                        share(4)
                pe.wait_ge(tap_ok, KC * (i + 1))
                for b, at in enumerate(SEG_BANKS):
                    pe.wait_ge(am_ok, 4 * i + b + 1)
                    if b == 3:
                        pe.wait_ge(z_ok, 2 * i + 1)
                    pe.matmul(bank[at][:, :], later, seg[:, 4 * b:4 * b + 4, :],
                              start=True, stop=True).then_inc(seg_mm, 1)
                pe.wait_ge(xc_ok, i + 1)
                for c in range(KX):
                    if c % 4 == 0:
                        pe.wait_ge(e_ok, 4 * i + 2 + c // 4)
                    m = pe.transpose(bank[XT_BANKS[c // 4]][:, (c % 4) * P:(c % 4 + 1) * P], xc[:, c, :], ident)
                    if c % 4 == 3:
                        m.then_inc(xT_mm, 1)
                pe.wait_ge(z_ok, 2 * i + 2)
                pe.transpose(bank[MISC][:, 0:P], xc[:, KX, :], ident)
                pe.matmul(bank[MISC][:, P:2 * P], xc[:, KX, :], xc[:, KX + 1, :], start=True, stop=True)
                pe.matmul(bank[MISC][:, 2 * P:2 * P + NH], upto, cur[:, 1, :], start=True, stop=True)
                pe.matmul(bank[MISC][:, 2 * P + NH:2 * P + 2 * NH], later, cur[:, 1, :], start=True, stop=True)
                pe.matmul(bank[MISC][:, 3 * P:3 * P + NH], ones, cur[:, 1, :], start=True, stop=True)\
                    .then_inc(cb_mm, 1)
                if first:
                    pe.wait_ge(zeroed, 3)
                else:
                    pe.wait_ge(st_ok, 2 * i)
                pe.wait_ge(e_ok, 4 * i + 4)
                for b in range(2):
                    pe.matmul(bank[YOFF_BANKS[b]][:, :], xc[:, KX + 1, :], state[:, b * BANK:(b + 1) * BANK],
                              start=True, stop=True).then_inc(yoff_mm, 1)
                share(5)
                share(6)

            def products(i, first, share):
                if first:
                    pe.wait_ge(const_made, KX)
                else:
                    pe.wait_ge(top1_ok, 3 * i)
                pe.wait_ge(xdt_ok, 2 * i + 2)
                pe.wait_ge(g_ok, i + 1)
                for c in range(KX):
                    at = bank[Y_BANKS[c // 4]]
                    col = (c % 4) * P
                    pe.matmul(at[:, col:col + P], xc[:, c, :], diag_d[:, c, :], start=(c % 4 == 0), stop=False,
                              skip_group_check=True)
                    for hh in (2 * c, 2 * c + 1):
                        m = pe.matmul(at[:, col + hh % 2 * HD:col + hh % 2 * HD + HD], seg[:, hh, :],
                                      xdt[:, hh * HD:(hh + 1) * HD], start=False,
                                      stop=(c % 4 == 3 and hh % 2 == 1), skip_group_check=True)
                    if c % 4 == 3:
                        m.then_inc(y_mm, 1)
                    if c == 3:
                        share(7)
                pe.wait_ge(dec_ok, 4 * i + 4)
                for b in range(2):
                    pe.wait_ge(xdec_ok, 2 * i + b + 1)
                    pe.matmul(bank[ST_BANKS[b]][:, :], btok, xdec[:, b * BANK:(b + 1) * BANK],
                              start=True, stop=True).then_inc(st_mm, 1)
                share(8)
                share(9)

            def out_proj(i, first, share):
                pe.wait_ge(y_ok, 2 * i + 2)
                for c in range(KX):
                    m = pe.transpose(bank[YT_BANKS[c // 4]][:, (c % 4) * P:(c % 4 + 1) * P], y[:, c * P:(c + 1) * P],
                                     ident)
                    if c % 4 == 3:
                        m.then_inc(yT_mm, 1)
                if first:
                    pe.wait_ge(const_made, 2 * KX)
                for c in range(KX):
                    if c % 4 == 0:
                        pe.wait_ge(yT_ok, 2 * i + c // 4 + 1)
                    m = pe.matmul(bank[OP][:, :], yT[:, c * P:(c + 1) * P], w_out[:, c, :],
                                  start=(c == 0), stop=(c == KX - 1))
                m.then_inc(op_mm, 1)
                share(10)

            def weighted(t, s):
                for k in PE_ROWS:
                    if k // GROUP == s:
                        n = PE_ROWS.index(k)
                        pe.wait_ge(diag_ok, len(PE_ROWS) * t + n + 1)
                        pe.matmul(bank[SUM][:, :], diag_c[:, n % DIAGS, :], ring[:, k % RING, DP:ROW],
                                  start=(n == 0), stop=(n == len(PE_ROWS) - 1)).then_inc(row_pe, 1)

            def tile(i, first, back, before, ahead):
                def ended(s):
                    if before:
                        weighted(i - 2, s)

                def share(s):
                    if back:
                        weighted(i - 1, s)

                if ahead:
                    xbc_proj(i + 1, False)
                ended(12)
                pe.wait_ge(x1_ok, i + 1)
                pe.wait_ge(st_ok, 2 * i + 2)
                for k in range(KD):
                    m = pe.transpose(bank[X1T][:, k * P:(k + 1) * P], x1_new[:, k * P:(k + 1) * P], ident)
                m.then_inc(x1T_mm, 1)
                if first:
                    pe.wait_ge(w_up_in, 16)
                pe.wait_ge(x1T_ok, i + 1)
                for c in range(KU):
                    if c == 12 and ahead:
                        pe.wait_ge(tap_ok, KC * (i + 1) + 4)
                    for k in range(KD):
                        m = pe.matmul(bank[UP_BANKS[c // 4]][:, (c % 4) * P:(c % 4 + 1) * P],
                                      w_up[:, k, c * P:(c + 1) * P], x1T[:, k, :], start=(k == 0), stop=(k == KD - 1))
                    if c % 4 == 3:
                        m.then_inc(h1_mm, 1)
                    if c == 3:
                        ended(13)
                if first:
                    pe.wait_ge(w_down_in, 16)
                if ahead:
                    pe.wait_ge(tap_ok, KC * (i + 1) + 8)
                for c in range(KU):
                    if c % 4 == 0:
                        pe.wait_ge(h1_ok, KU * i + c + 4)
                    m = pe.matmul(bank[DOWN][:, 0:DP], h1T[:, c, :], w_down[:, c, :],
                                  start=(c == 0), stop=(c == KU - 1))
                m.then_inc(hp_mm, 1)
                share(0)
                share(1)
                pe.wait_ge(h_ok, i + 1)
                if ahead:
                    pe.wait_ge(tap_ok, KC * (i + 2))
                for c in range(KP):
                    m = pe.transpose(bank[HT][:, c * P:(c + 1) * P], h[:, c * P:(c + 1) * P], ident)
                m.then_inc(hT_mm, 1)
                pe.wait_ge(hT_ok, i + 1)
                for b in range(2):
                    for c in range(KP):
                        m = pe.matmul(bank[SIM_BANKS[b]][:, :], hT[:, c, :], w_key[:, c, b * BANK:(b + 1) * BANK],
                                      start=(c == 0), stop=(c == KP - 1))
                    if b == 0:
                        share(2)
                m.then_inc(sim_mm, 1)
                share(3)
                if ahead:
                    lead(i + 1, False, share)
                    products(i + 1, False, share)
                    out_proj(i + 1, False, share)
                    share(11)
                else:
                    for g in range(4, STEPS):
                        share(g)

            xbc_proj(0, True)
            lead(0, True, lambda s: None)
            products(0, True, lambda s: None)
            out_proj(0, True, lambda s: None)
            tile(0, True, False, False, True)
            tile(1, False, True, False, True)
            with pe.Fori(2, NT - 1) as i:
                tile(i, False, True, True, True)
            tile(NT - 1, False, True, True, False)
            for g in range(STEPS):
                weighted(NT - 1, g)

        @block.scalar
        def _(act):
            w_in_k = W_in.rearrange("(k p) n -> p k n", p=P)
            act.dma_start(w_in[:, :, DPROJ - NH:DPROJ], w_in_k[:, :, DPROJ - NH:DPROJ]).then_inc(wdt_in, 16)
            act.dma_start(small[:, 0, :], dt_bias).then_inc(w_small, 16)
            act.dma_start(small[:, 1, :], A_log).then_inc(w_small, 16)
            act.dma_start(cst[:, :, :], consts).then_inc(w_small, 16)
            act.dma_start(iota[:, :], iota8).then_inc(w_small, 16)
            act.dma_start(taps[:, :, :], conv_w).then_inc(w_small, 16)
            act.dma_start(cbias[:, :], conv_b).then_inc(w_small, 16)
            act.dma_start(dcol[:, :], D_cols).then_inc(w_small, 16)
            act.dma_start(ncol[:, :], norm_cols).then_inc(w_small, 16)
            act.dma_start(bup[:, :], b_up).then_inc(w_small, 16)
            act.dma_start(bdown[:, :], b_down).then_inc(w_small, 16)
            act.dma_start(w_in[:, :, 0:DPROJ - NH], w_in_k[:, :, 0:DPROJ - NH]).then_inc(w_in_in, 16)
            act.wait_ge(dt_mm, NT // DTB)
            act.dma_start(w_out[:, :, :], W_out.rearrange("(k p) n -> p k n", p=P)).then_inc(w_out_in, 16)
            act.dma_start(w_up[:, :, :], W_upT.rearrange("(k p) n -> p k n", p=P)).then_inc(w_up_in, 16)
            act.dma_start(w_down[:, :, :], W_downT.rearrange("(k p) n -> p k n", p=P)).then_inc(w_down_in, 16)
            act.wait_ge(w_small, 160)
            act.activation(small[:, 2, :], small[:, 1, :], ACT.Exp).then_inc(expa_made, 1)
            act.wait_ge(dt_raw, NT // DTB)
            sp_e = acc[:, 0, :]
            act.activation(sp_e, steps[:, :, :].rearrange("p a b -> p (a b)"), ACT.Abs).then_inc(dt_act, 1)
            act.wait_ge(dt_act, 1)
            act.activation(sp_e, sp_e, ACT.Exp, scale=-1.0).then_inc(dt_act, 1)
            act.wait_ge(zeroed, 3)

            def coefs(t, g):
                act.wait_ge(zp_ok, STEPS * t + g + 1)
                act.activation(coef[:, g * GROUP:(g + 1) * GROUP], zp[:, g * GROUP:(g + 1) * GROUP], ACT.Silu)\
                    .then_inc(coef_ok, 1)
                for k in PE_ROWS:
                    if k // GROUP == g:
                        act.wait_ge(coef_ok, STEPS * t + g + 1)
                        n = PE_ROWS.index(k)
                        if n >= DIAGS:
                            act.wait_ge(row_pe, len(PE_ROWS) * t + n - DIAGS + 1)
                        act.activation(diag_c[:, n % DIAGS, :], ident, ACT.Copy, scale=coef[:, k:k + 1])\
                            .then_inc(diag_ok, 1)

            def history(i):
                act.wait_ge(conv_ok, KC * 3 * i)
                act.activation(raw[:, :, 0:TAPS - 1], raw[:, :, P:P + TAPS - 1], ACT.Copy).then_inc(hist_ok, 1)
                act.wait_ge(hist_ok, i)
                act.wait_ge(y_mm, 2 * i)

            def inputs(i, b):
                n = min(4, KC - 4 * b)
                at = bank[XBC_BANKS[b]]
                act.wait_ge(xbc_mm, 3 * i + b + 1)
                act.activation(raw[:, 4 * b:4 * b + n, TAPS - 1:],
                               at[:, 0:n * P].rearrange("p (a c) -> p a c", a=n), ACT.Copy).then_inc(raw_ok, 1)
                for c in range(4 * b, 4 * b + n):
                    act.activation(xc[:, c, :], at[:, (c % 4) * P:(c % 4 + 1) * P], ACT.Identity,
                                   bias=cbias[:, c:c + 1], scale=taps[:, c, TAPS - 1:TAPS]).then_inc(tap_ok, 1)

            def conv_silu(i):
                act.wait_ge(conv_ok, KC * 3 * (i + 1))
                act.activation(xc[:, :, :], xc[:, :, :], ACT.Silu).then_inc(xc_ok, 1)

            def masked_steps(i, which, first):
                act.wait_ge(cur_ok, 2 * i + 2)
                if not first:
                    act.wait_ge(hp_mm, i)
                for hh in which:
                    m = act.activation(seg[:, hh, :], upto, ACT.Copy, scale=cur[:, 1, hh:hh + 1])
                    if hh % 4 == 3:
                        m.then_inc(am_ok, 1)

            def gates(i, first):
                for b in range(2):
                    act.wait_ge(z_mm, 2 * i + b + 1)
                    if b == 0 and not first:
                        act.wait_ge(sim_mm, i)
                    act.activation(zs[:, b * BANK:(b + 1) * BANK], bank[Z_BANKS[b]][:, :], ACT.Silu).then_inc(z_ok, 1)

            def decays(i, first):
                for b, at in enumerate(SEG_BANKS):
                    act.wait_ge(seg_mm, 4 * i + b + 1)
                    act.activation(seg[:, 4 * b:4 * b + 4, :],
                                   bank[at][:, :].rearrange("p (a c) -> p a c", a=4), ACT.Exp).then_inc(e_ok, 1)
                act.wait_ge(cb_mm, i + 1)
                act.activation(decay[:, 0, :], bank[MISC][:, 2 * P:2 * P + NH], ACT.Exp).then_inc(dec_ok, 1)
                act.activation(decay[:, 1, :], bank[MISC][:, 3 * P:3 * P + NH], ACT.Exp).then_inc(dec_ok, 1)
                act.activation(decay[:, 2, :], bank[MISC][:, 2 * P + NH:2 * P + 2 * NH], ACT.Exp).then_inc(dec_ok, 1)
                if not first:
                    act.wait_ge(st_mm, 2 * i)
                    act.wait_ge(g_ok, i)
                act.activation(bcb[:, :, :], bank[MISC][:, 0:2 * P].rearrange("p (a c) -> p a c", a=2), ACT.Copy)\
                    .then_inc(dec_ok, 1)

            def end_decay(i, which):
                act.wait_ge(xdt_ok, 2 * i + 2)
                act.wait_ge(dec_ok, 4 * i + 3)
                for hh in which:
                    m = act.activation(xdec[:, hh * HD:(hh + 1) * HD], xdt[:, hh * HD:(hh + 1) * HD], ACT.Copy,
                                       scale=decay[:, 2, hh:hh + 1])
                m.then_inc(xdec_ok, 1)

            def state_decay(i, which):
                act.wait_ge(yoff_mm, 2 * i + 2)
                act.wait_ge(dec_ok, 4 * i + 2)
                for hh in which:
                    m = act.activation(state[:, hh * HD:(hh + 1) * HD], state[:, hh * HD:(hh + 1) * HD], ACT.Copy,
                                       scale=decay[:, 1, hh:hh + 1])
                m.then_inc(dcy_ok, 1)

            def turn_y(i):
                for b in range(2):
                    act.wait_ge(yT_mm, 2 * i + b + 1)
                    if b == 0:
                        act.wait_ge(st_mm, 2 * i + 2)
                    act.activation(yT[:, b * BANK:(b + 1) * BANK], bank[YT_BANKS[b]][:, :], ACT.Identity).then_inc(yT_ok, 1)

            def gated_squares(i):
                act.activation(y[:, :], y[:, :], ACT.Square, accum_out=sm[:, 0:1]).then_inc(sq_ok, 1)

            def gated_rms(i):
                act.wait_ge(sq_ok, i + 1)
                act.activation(sm[:, 1:2], sm[:, 0:1], ACT.Sqrt, scale=1.0 / DI, bias=epsc[:, :]).then_inc(rms_ok, 1)

            def deviation(i):
                act.wait_ge(bn_ok, 4 * i + 3)
                act.activation(sm[:, 3:4], mv[:, 1:2], ACT.Sqrt, bias=epsc[:, :]).then_inc(ln_ok, 1)

            def turn_x1(i):
                act.wait_ge(x1T_mm, i + 1)
                act.activation(x1T, bank[X1T][:, :].rearrange("p (a c) -> p a c", a=KD), ACT.Copy).then_inc(x1T_ok, 1)

            def up_silu(i, b):
                act.wait_ge(h1_mm, 4 * i + b + 1)
                for c in range(4 * b, 4 * b + 4):
                    act.activation(h1T[:, c, :], bank[UP_BANKS[b]][:, (c % 4) * P:(c % 4 + 1) * P], ACT.Silu,
                                   bias=bup[:, c:c + 1]).then_inc(h1_ok, 1)

            def turn_h(i):
                act.wait_ge(hT_mm, i + 1)
                act.activation(hT, bank[HT][:, 0:DP].rearrange("p (a c) -> p a c", a=KP), ACT.Copy).then_inc(hT_ok, 1)

            def soft_exp(i):
                act.wait_ge(soft_ok, 4 * i + 1)
                act.activation(raised[:, :, :], raised[:, :, :], ACT.Exp).then_inc(exp_ok, 1)

            def back_sqrt(t):
                act.wait_ge(sum_ok, 4 * t + 4)
                act.activation(smb[:, 0:1], mvb[:, 1:2], ACT.Sqrt, bias=epsc[:, :]).then_inc(ln2_ok, 1)

            def hand_over(i, first):
                act.wait_ge(h_ok, i + 1)
                if not first:
                    act.wait_ge(dot_ok, PICKS * i)
                act.activation(hcur[:, :], h[:, :], ACT.Copy).then_inc(hcur_ok, 1)

            def keep_x1(i, back):
                act.wait_ge(saved_ok, i + 1)
                if back:
                    act.wait_ge(o_ok, i)
                act.activation(acc[:, 0, :], x1[:, :], ACT.Copy).then_inc(kept_ok, 1)

            def save_x1(i, first):
                act.wait_ge(x1_ok, i + 1)
                if not first:
                    act.wait_ge(kept_ok, i)
                act.activation(x1[:, :], x1_new, ACT.Copy).then_inc(saved_ok, 1)

            def tile(i, first, back, before, ahead):
                def share(s):
                    if back:
                        coefs(i - 1, s)

                if ahead:
                    history(i + 1)
                    inputs(i + 1, 0)
                    inputs(i + 1, 1)
                if before:
                    back_sqrt(i - 2)
                if not first:
                    keep_x1(i - 1, before)
                if ahead:
                    inputs(i + 1, 2)
                share(0)
                up_silu(i, 0)
                up_silu(i, 1)
                share(1)
                up_silu(i, 2)
                up_silu(i, 3)
                share(2)
                save_x1(i, first)
                turn_h(i)
                if ahead:
                    masked_steps(i + 1, range(NH // 2), False)
                share(3)
                if ahead:
                    conv_silu(i + 1)
                    masked_steps(i + 1, range(NH // 2, NH), False)
                share(4)
                if ahead:
                    gates(i + 1, False)
                    decays(i + 1, False)
                share(5)
                share(6)
                if ahead:
                    end_decay(i + 1, range(NH // 2))
                soft_exp(i)
                share(7)
                if ahead:
                    end_decay(i + 1, range(NH // 2, NH))
                share(8)
                if ahead:
                    state_decay(i + 1, range(NH // 2))
                share(9)
                if ahead:
                    state_decay(i + 1, range(NH // 2, NH))
                if ahead:
                    turn_y(i + 1)
                    gated_squares(i + 1)
                share(10)
                if ahead:
                    gated_rms(i + 1)
                share(11)
                share(12)
                if ahead:
                    deviation(i + 1)
                share(13)
                share(14)
                if ahead:
                    turn_x1(i + 1)
                share(15)
                hand_over(i, first)
                act.activation(sm[:, 5:6], epsc[:, :], ACT.Sqrt).then_inc(table_in, 1)

            for b in range(3):
                inputs(0, b)
            masked_steps(0, range(NH), True)
            conv_silu(0)
            gates(0, True)
            decays(0, True)
            for half in (range(NH // 2), range(NH // 2, NH)):
                end_decay(0, half)
                state_decay(0, half)
            turn_y(0)
            gated_squares(0)
            gated_rms(0)
            deviation(0)
            turn_x1(0)
            tile(0, True, False, False, True)
            tile(1, False, True, False, True)
            with act.Fori(2, NT - 1) as i:
                tile(i, False, True, True, True)
            tile(NT - 1, False, True, True, False)
            back_sqrt(NT - 2)
            keep_x1(NT - 1, True)
            for g in range(STEPS):
                coefs(NT - 1, g)
            back_sqrt(NT - 1)

        @block.vector
        def _(dve):
            for c in range(2 * KP):
                dve.wait_ge(keyw_mm, c + 1)
                dve.tensor_copy(w_key[:, c // 2, (c % 2) * BANK:(c % 2 + 1) * BANK], bank[c][:, :]).then_inc(keyw_out, 1)
            dve.wait_ge(w_small, 160)
            for c in range(KX):
                dve.tensor_scalar(diag_d[:, c, :], ident, dcol[:, c:c + 1], None, ALU.mult).then_inc(const_made, 1)
            sp_x = steps[:, :, :].rearrange("p a b -> p (a b)")
            sp_e, sp_p, sp_r = acc[:, 0, :], acc[:, 1, :], x1[:, :]
            for b in range(NT // DTB):
                dve.wait_ge(dt_mm, b + 1)
                dve.tensor_tensor(steps[:, b * DTB:(b + 1) * DTB, :],
                                  bank[4 + b][:, 0:DTB * NH].rearrange("p (t n) -> p t n", n=NH),
                                  small[:, 0:1, :].to_broadcast([P, DTB, NH]), ALU.add).then_inc(dt_raw, 1)
            dve.wait_ge(dt_act, 2)
            dve.tensor_scalar(sp_r, sp_e, 2.0, None, ALU.add).then_inc(dt_dve, 1)
            dve.wait_ge(dt_dve, 1)
            dve.reciprocal(sp_r, sp_r).then_inc(dt_dve, 1)
            dve.wait_ge(dt_dve, 2)
            dve.tensor_tensor(sp_r, sp_e, sp_r, ALU.mult).then_inc(dt_dve, 1)
            dve.wait_ge(dt_dve, 3)
            dve.tensor_tensor(sp_e, sp_r, sp_r, ALU.mult).then_inc(dt_dve, 1)
            dve.wait_ge(dt_dve, 4)
            dve.tensor_scalar(sp_p, sp_e, 1.0 / 17, None, ALU.mult).then_inc(dt_dve, 1)
            for n, odd in enumerate((15, 13, 11, 9, 7, 5, 3)):
                dve.wait_ge(dt_dve, 5 + n)
                dve.scalar_tensor_tensor(out=sp_p, in0=sp_p, scalar=1.0 / odd, in1=sp_e, op0=ALU.add, op1=ALU.mult)\
                    .then_inc(dt_dve, 1)
            dve.wait_ge(dt_dve, 12)
            dve.scalar_tensor_tensor(out=sp_p, in0=sp_p, scalar=1.0, in1=sp_r, op0=ALU.add, op1=ALU.mult)\
                .then_inc(dt_dve, 1)
            dve.tensor_scalar(sp_x, sp_x, 0.0, 0.5, ALU.max, ALU.mult).then_inc(dt_dve, 1)
            dve.wait_ge(dt_dve, 14)
            dve.tensor_tensor(sp_p, sp_p, sp_x, ALU.add).then_inc(dt_dve, 1)
            dve.wait_ge(dt_dve, 15)
            dve.tensor_scalar(sp_x, sp_p, 2.0, None, ALU.mult).then_inc(dt_dve, 1)
            dve.wait_ge(dt_dve, 16)
            dve.wait_ge(expa_made, 1)
            dve.wait_ge(zeroed, 3)

            def heads(ap):
                return ap.rearrange("p (n c) -> p n c", c=HD)

            def time_steps(i):
                dt_i = steps[:, bass.ds(i, 1), :]
                dve.tensor_scalar(cur[:, 0:1, :], dt_i, 1.0, None, ALU.mult).then_inc(cur_ok, 1)
                dve.scalar_tensor_tensor(out=cur[:, 1:2, :], in0=dt_i, scalar=-1.0, in1=small[:, 2:3, :],
                                         op0=ALU.mult, op1=ALU.mult).then_inc(cur_ok, 1)

            def convolve(i, j):
                for c in range(KC):
                    if j == 0:
                        dve.wait_ge(tap_ok, KC * i + c + 1)
                    else:
                        dve.wait_ge(conv_ok, KC * (3 * i + j - 1) + c + 1)
                    dve.scalar_tensor_tensor(out=xc[:, c, :], in0=raw[:, c, j:j + P], scalar=taps[:, c, j:j + 1],
                                             in1=xc[:, c, :], op0=ALU.mult, op1=ALU.add).then_inc(conv_ok, 1)

            def scan_in(i, between=lambda: None):
                for b in range(2):
                    dve.wait_ge(xT_mm, 2 * i + b + 1)
                    dve.tensor_tensor(heads(xdt[:, b * BANK:(b + 1) * BANK]), heads(bank[XT_BANKS[b]][:, :]),
                                      cur[:, 0, 8 * b:8 * b + 8].unsqueeze(2).to_broadcast([P, 8, HD]),
                                      ALU.mult).then_inc(xdt_ok, 1)
                between()
                dve.wait_ge(dec_ok, 4 * i + 4)
                dve.tensor_tensor(cbm, cbm, upto, ALU.mult).then_inc(cbm_ok, 1)
                dve.wait_ge(e_ok, 4 * i + 4)
                dve.wait_ge(cbm_ok, i + 1)
                dve.tensor_tensor(seg[:, :, :], seg[:, :, :], cbm.unsqueeze(1).to_broadcast([P, NH, P]),
                                  ALU.mult).then_inc(g_ok, 1)

            def scan_out(i, between=lambda: None):
                dve.wait_ge(yoff_mm, 2 * i + 2)
                between()
                dve.wait_ge(xdec_ok, 2 * i + 2)
                for b in range(2):
                    dve.wait_ge(y_mm, 2 * i + 2)
                    dve.tensor_tensor(heads(y[:, b * BANK:(b + 1) * BANK]), heads(bank[YOFF_BANKS[b]][:, :]),
                                      decay[:, 0, 8 * b:8 * b + 8].unsqueeze(2).to_broadcast([P, 8, HD]),
                                      ALU.mult).then_inc(yoff_ok, 1)
                for b in range(2):
                    dve.wait_ge(yoff_ok, 2 * i + b + 1)
                    dve.tensor_tensor(y[:, b * BANK:(b + 1) * BANK], y[:, b * BANK:(b + 1) * BANK], bank[Y_BANKS[b]][:, :],
                                      ALU.add).then_inc(y_half, 1)
                dve.wait_ge(z_ok, 2 * i + 2)
                for b in range(2):
                    dve.wait_ge(y_half, 2 * i + b + 1)
                    dve.tensor_tensor(y[:, b * BANK:(b + 1) * BANK], y[:, b * BANK:(b + 1) * BANK],
                                      zs[:, b * BANK:(b + 1) * BANK], ALU.mult).then_inc(y_ok, 1)

            def new_state(i):
                dve.wait_ge(dcy_ok, 2 * i + 2)
                for b in range(2):
                    dve.wait_ge(st_mm, 2 * i + b + 1)
                    dve.tensor_tensor(state[:, b * BANK:(b + 1) * BANK], state[:, b * BANK:(b + 1) * BANK],
                                      bank[ST_BANKS[b]][:, :], ALU.add).then_inc(st_ok, 1)

            def residual(i):
                dve.wait_ge(rms_ok, i + 1)
                dve.reciprocal(sm[:, 2:3], sm[:, 1:2]).then_inc(rr_ok, 1)
                dve.wait_ge(rr_ok, i + 1)
                dve.wait_ge(op_mm, i + 1)
                dve.wait_ge(utok_in, 16 * i + 16)
                dve.scalar_tensor_tensor(out=x1_new, in0=bank[OP][:, :], scalar=sm[:, 2:3], in1=u_tok,
                                         op0=ALU.mult, op1=ALU.add).then_inc(bn_ok, 1)
                dve.wait_ge(bn_ok, 4 * i + 1)
                dve.bn_stats(st6[:, :], x1_new).then_inc(bn_ok, 1)
                dve.wait_ge(bn_ok, 4 * i + 2)
                dve.sem_inc(dve_fence, 1)
                dve.bn_aggr(mv[:, :], st6[:, :]).then_inc(bn_ok, 1)

            def norm1(i):
                dve.wait_ge(ln_ok, i + 1)
                dve.reciprocal(sm[:, 4:5], sm[:, 3:4]).then_inc(bn_ok, 1)
                dve.wait_ge(bn_ok, 4 * i + 4)
                dve.tensor_scalar(x1_new, x1_new, mv[:, 0:1], sm[:, 4:5], ALU.subtract, ALU.mult).then_inc(x1_ok, 1)

            def private(i):
                dve.wait_ge(hp_mm, i + 1)
                dve.tensor_tensor(h[:, :], bank[DOWN][:, 0:DP], bdown[:, :], ALU.add).then_inc(h_ok, 1)

            def top_halves(i, between):
                dve.wait_ge(sim_mm, i + 1)
                dve.sem_inc(dve_fence, 1)
                for g in range(NG):
                    m = dve.max(out=v1[:, g, :], in_=bank[SIM_BANKS[g // 8]][:, (g % 8) * NK:(g % 8 + 1) * NK])
                m.then_inc(top1_ok, 1)
                between()
                dve.wait_ge(top1_ok, 3 * i + 1)
                dve.sem_inc(dve_fence, 1)
                for g in range(NG):
                    m = dve.max_index(i1[:, g, :], v1[:, g, :], bank[SIM_BANKS[g // 8]][:, (g % 8) * NK:(g % 8 + 1) * NK])
                m.then_inc(top1_ok, 1)
                dve.wait_ge(saved_ok, i + 1)
                dve.tensor_tensor(allsc.rearrange("p n (a b) -> p n a b", a=TOP),
                                  v1[:, 0:EH, :].unsqueeze(3).to_broadcast([P, EH, TOP, TOP]),
                                  v1[:, EH:NG, :].unsqueeze(2).to_broadcast([P, EH, TOP, TOP]), ALU.add).then_inc(top1_ok, 1)

            def top_pairs(i):
                dve.wait_ge(top1_ok, 3 * i + 3)
                dve.sem_inc(dve_fence, 1)
                for n in range(EH):
                    m = dve.max(out=v2[:, n, :], in_=allsc[:, n, :])
                m.then_inc(top2_ok, 1)
                dve.wait_ge(top2_ok, 4 * i + 1)
                dve.sem_inc(dve_fence, 1)
                for n in range(EH):
                    m = dve.max_index(pk[:, n, :], v2[:, n, :], allsc[:, n, :])
                m.then_inc(top2_ok, 1)
                dve.wait_ge(top2_ok, 4 * i + 2)
                pk_v = pk[:, :, :].rearrange("p a b -> p (a b)")
                dve.tensor_scalar(bk[:, :], pk_v, TOP - 1, None, ALU.bitwise_and).then_inc(top2_ok, 1)
                dve.wait_ge(top2_ok, 4 * i + 3)
                dve.tensor_scalar(pk_v, pk_v, 3, None, ALU.logical_shift_right).then_inc(top2_ok, 1)
                hot_x = allsc.rearrange("p n (k a) -> p n k a", a=TOP)
                hot_y = hot.rearrange("p (n k) a -> p n k a", n=EH)
                for place, one in ((pk_v, hot_x), (bk[:, :], hot_y)):
                    dve.wait_ge(top2_ok, 4 * i + 4)
                    dve.tensor_tensor(one.rearrange("p n k a -> p (n k) a"),
                                      place.unsqueeze(2).to_broadcast([P, PICKS, TOP]),
                                      iota[:, :].unsqueeze(1).to_broadcast([P, PICKS, TOP]),
                                      ALU.is_equal).then_inc(hot_ok, 1)
                for n, one in enumerate((hot_x, hot_y)):
                    dve.wait_ge(hot_ok, 2 * i + n + 1)
                    dve.tensor_tensor(one, one, i1[:, n * EH:(n + 1) * EH, :].unsqueeze(2).to_broadcast([P, EH, TOP, TOP]),
                                      ALU.mult).then_inc(pick_ok, 1)
                for n, one in enumerate((hot_x, hot_y)):
                    dve.wait_ge(pick_ok, 2 * i + n + 1)
                    dve.tensor_reduce(ixy[:, n, :], one.rearrange("p n k a -> p (n k) a"), AX.X, ALU.add).then_inc(ixy_ok, 1)
                dve.wait_ge(ixy_ok, 2 * i + 2)
                dve.scalar_tensor_tensor(out=idx[:, bass.ds(i % 2, 1), :], in0=ixy[:, 0:1, :], scalar=float(NK), in1=ixy[:, 1:2, :],
                                         op0=ALU.mult, op1=ALU.add).then_inc(idx_ok, 1)

            def shifted(i):
                dve.wait_ge(top2_ok, 4 * i + 1)
                dve.wait_ge(idx_ok, i + 1)
                dve.tensor_tensor(raised[:, :, :], v2[:, :, :], v2[:, :, 0:1].to_broadcast([P, EH, TOP]), ALU.subtract)\
                    .then_inc(soft_ok, 1)

            def softmax(i, first):
                dve.wait_ge(exp_ok, i + 1)
                dve.tensor_reduce(psm[:, 0, :], raised[:, :, :], AX.X, ALU.add).then_inc(soft_ok, 1)
                dve.wait_ge(soft_ok, 4 * i + 2)
                dve.reciprocal(psm[:, 1, :], psm[:, 0, :]).then_inc(soft_ok, 1)
                dve.wait_ge(soft_ok, 4 * i + 3)
                if not first:
                    dve.wait_ge(zp_ok, STEPS * i)
                dve.tensor_tensor(prob[:, :, :], raised[:, :, :], psm[:, 1, :].unsqueeze(2).to_broadcast([P, EH, TOP]),
                                  ALU.mult).then_inc(soft_ok, 1)

            def uses(k):
                return len(range(k % RING, PICKS, RING))

            def dots_of(t, g):
                if g == 0:
                    dve.wait_ge(hcur_ok, t + 1)
                for k in range(g * GROUP, (g + 1) * GROUP):
                    dve.wait_ge(row_in[k % RING], 16 * (uses(k) * t + k // RING + 1))
                    dve.scalar_tensor_tensor(out=ring[:, k % RING, 0:DP], in0=ring[:, k % RING, 0:DP], scalar=1.0,
                                             in1=hcur[:, :], op0=ALU.mult, op1=ALU.mult,
                                             accum_out=dots[:, k:k + 1]).then_inc(dot_ok, 1)

            def times_prob(t, g):
                dve.wait_ge(dot_ok, PICKS * t + (g + 1) * GROUP)
                if g == 0:
                    dve.wait_ge(soft_ok, 4 * t + 4)
                at = g * GROUP
                dve.tensor_tensor(zp[:, at:at + GROUP], dots[:, at:at + GROUP],
                                  prob[:, at // TOP, at % TOP:at % TOP + GROUP], ALU.mult).then_inc(zp_ok, 1)

            def weigh(t, g):
                dve.wait_ge(coef_ok, STEPS * t + g + 1)
                for k in DVE_ROWS:
                    if k // GROUP != g:
                        continue
                    n = DVE_ROWS.index(k)
                    half = n % 2 if n >= FIRST_ODD else 0
                    before = n - 1 if n < FIRST_ODD else n - 2
                    if n == 0:
                        dve.wait_ge(kept_ok, t + 1)
                    elif n != FIRST_ODD:
                        dve.wait_ge(row_used, len(DVE_ROWS) * t + before + 1)
                    if n == FIRST_ODD:
                        dve.wait_ge(out_done, 16 * t + 16)
                    if n == FIRST_ODD:
                        dve.tensor_scalar(acc[:, 1, :], ring[:, k % RING, DP:ROW], coef[:, k:k + 1], None, ALU.mult)\
                            .then_inc(row_used, 1)
                    else:
                        dve.scalar_tensor_tensor(out=acc[:, half, :], in0=ring[:, k % RING, DP:ROW],
                                                 scalar=coef[:, k:k + 1], in1=acc[:, half, :],
                                                 op0=ALU.mult, op1=ALU.add).then_inc(row_used, 1)

            def back_stats(t):
                dve.wait_ge(row_used, len(DVE_ROWS) * (t + 1))
                dve.tensor_tensor(acc[:, 0, :], acc[:, 0, :], acc[:, 1, :], ALU.add).then_inc(sum_ok, 1)
                dve.wait_ge(sum_ok, 4 * t + 1)
                dve.wait_ge(row_pe, len(PE_ROWS) * (t + 1))
                dve.tensor_tensor(acc[:, 0, :], acc[:, 0, :], bank[SUM][:, :], ALU.add).then_inc(sum_ok, 1)
                dve.wait_ge(sum_ok, 4 * t + 2)
                dve.bn_stats(st6b[:, :], acc[:, 0, :]).then_inc(sum_ok, 1)
                dve.wait_ge(sum_ok, 4 * t + 3)
                dve.sem_inc(dve_fence, 1)
                dve.bn_aggr(mvb[:, :], st6b[:, :]).then_inc(sum_ok, 1)

            def back_norm(t):
                dve.wait_ge(ln2_ok, t + 1)
                dve.reciprocal(smb[:, 1:2], smb[:, 0:1]).then_inc(r2_ok, 1)
                dve.wait_ge(r2_ok, t + 1)
                dve.tensor_scalar(obuf, acc[:, 0, :], mvb[:, 0:1], smb[:, 1:2], ALU.subtract, ALU.mult)\
                    .then_inc(o_ok, 1)

            def tile(i, first, back, ahead):
                def step(*which):
                    for g in which:
                        if back:
                            dots_of(i - 1, g)
                            if g > 0 and g - 1 not in EARLY:
                                weigh(i - 1, g - 1)
                            times_prob(i - 1, g)

                def early(g):
                    return (lambda: weigh(i - 1, g)) if back else (lambda: None)

                step(0, 1)
                if ahead:
                    time_steps(i + 1)
                    convolve(i + 1, 0)
                step(2)
                private(i)
                if ahead:
                    convolve(i + 1, 1)
                step(3)
                if ahead:
                    convolve(i + 1, 2)
                step(4)
                top_halves(i, early(4))
                step(5)
                top_pairs(i)
                shifted(i)
                step(6)
                if ahead:
                    scan_in(i + 1, early(6))
                else:
                    early(6)()
                step(7, 8, 9)
                if ahead:
                    scan_out(i + 1, early(9))
                else:
                    early(9)()
                step(10)
                if ahead:
                    new_state(i + 1)
                step(11, 12)
                if ahead:
                    residual(i + 1)
                step(13)
                if ahead:
                    norm1(i + 1)
                step(14, 15)
                softmax(i, first)
                if back:
                    weigh(i - 1, STEPS - 1)
                    back_stats(i - 1)
                    back_norm(i - 1)

            time_steps(0)
            for j in range(TAPS - 1):
                convolve(0, j)
            dve.wait_ge(w_out_in, 16)
            for c in range(KX):
                dve.tensor_scalar(w_out[:, c, :], w_out[:, c, :], ncol[:, c:c + 1], None, ALU.mult)\
                    .then_inc(const_made, 1)
            scan_in(0)
            scan_out(0)
            new_state(0)
            residual(0)
            norm1(0)
            tile(0, True, False, True)
            with dve.Fori(1, NT - 1) as i:
                tile(i, False, True, True)
            tile(NT - 1, False, True, False)
            dots_of(NT - 1, 0)
            times_prob(NT - 1, 0)
            for g in range(1, STEPS):
                dots_of(NT - 1, g)
                weigh(NT - 1, g - 1)
                times_prob(NT - 1, g)
            weigh(NT - 1, STEPS - 1)
            back_stats(NT - 1)
            back_norm(NT - 1)


def kernel(L0_attn_u, L0_attn_W_in, L0_attn_conv_w, L0_attn_conv_b, L0_attn_dt_bias, L0_attn_A_log, L0_attn_D,
           L0_attn_norm_scale, L0_attn_W_out, L0_ffn_W_up, L0_ffn_b_up, L0_ffn_W_down, L0_ffn_b_down,
           L0_ffn_W_q, L0_ffn_keys, L0_ffn_down_embed, L0_ffn_up_embed):
    import concourse.bacc as bacc
    from concourse.bass_utils import run_bass_kernel_spmd

    def a(x):
        return np.asarray(x)

    def c(x):
        return np.ascontiguousarray(x)

    def rows(x):
        return c(np.broadcast_to(a(x)[None, :], (P, x.shape[0])))

    def cols(x, n):
        return c(a(x).reshape(n, P).T)

    u = a(L0_attn_u).reshape(NT, P, D)
    q = np.arange(P)
    consts = np.stack([q[:, None] == q[None, :], q[:, None] > q[None, :], q[:, None] <= q[None, :],
                       q[:, None] >= 0 * q[None, :]], 1).astype(np.float32)
    arrays = {
        "uT": c(u.reshape(NT, P, KD, P).transpose(0, 3, 2, 1).reshape(NT, P, D)),
        "u": c(u),
        "W_in": c(a(L0_attn_W_in)),
        "W_out": c(a(L0_attn_W_out)),
        "W_upT": c(a(L0_ffn_W_up).T),
        "W_downT": c(a(L0_ffn_W_down).T),
        "W_q": c(a(L0_ffn_W_q)),
        "keysT": c(a(L0_ffn_keys).transpose(3, 2, 0, 1).reshape(HALF, NG, NK)),
        "embed": c(np.concatenate([a(L0_ffn_down_embed), a(L0_ffn_up_embed)], 1)),
        "consts": consts,
        "iota8": c(np.broadcast_to(np.arange(TOP, dtype=np.float32), (P, TOP))),
        "conv_w": c(a(L0_attn_conv_w).reshape(TAPS, KC, P).transpose(2, 1, 0)),
        "conv_b": cols(L0_attn_conv_b, KC),
        "dt_bias": rows(L0_attn_dt_bias),
        "A_log": rows(L0_attn_A_log),
        "D_cols": cols(np.repeat(a(L0_attn_D), HD), KX),
        "norm_cols": cols(L0_attn_norm_scale, KX),
        "b_up": cols(L0_ffn_b_up, KU),
        "b_down": rows(L0_ffn_b_down),
    }
    nc = bacc.Bacc("TRN2", target_bir_lowering=False, num_devices=1)
    args = [nc.dram_tensor(n, x.shape, mybir.dt.from_np(x.dtype), kind="ExternalInput").ap() for n, x in arrays.items()]
    args.append(nc.dram_tensor("out", (NT, P, D), F32, kind="ExternalOutput").ap())
    build(nc, *args)
    r = run_bass_kernel_spmd(nc, [arrays], core_ids=[0])
    return r.results[0]["out"].reshape(1, T, D)
```
